# Optimizing a Trainium2 kernel written in Bass

```python
import numpy as np
import jax
import jax.numpy as jnp

def _softmax(x, axis=-1):
    return jax.nn.softmax(x, axis=axis)

def _gelu(x):
    return jax.nn.gelu(x, approximate=True)

def _silu(x):
    return jax.nn.silu(x)

def _sigmoid(x):
    return jax.nn.sigmoid(x)

def _layernorm(x, axis=-1, eps=1e-05):
    m = jnp.mean(x, axis=axis, keepdims=True)
    v = jnp.var(x, axis=axis, keepdims=True)
    return (x - m) / jnp.sqrt(v + eps)

def _scatter_add(tgt, idx, src, axis=0):
    return tgt.at[idx].add(src)

def _segment_sum(src, seg, n):
    return jax.ops.segment_sum(src, seg, n)
kernel_name = 'mk_adj_preln_d1_adj_r2_de90ef'

def setup_inputs(seed: int=0):
    np.random.seed(seed)
    _w = jnp.asarray

    def _rec_inputs():
        import jax
        import jax.numpy as jnp
        _gk = jax.random.key(seed)
        x = -0.0005207 + 1.001 * jax.random.normal(jax.random.fold_in(_gk, 1), (4096, 256), jnp.float32)
        _w = (1.0 + jnp.arange(4096, dtype=jnp.float32)) ** (-0.5)
        _w = _w / _w.mean()
        _pij = jnp.clip(0.000488281 * _w[:, None] * _w[None, :], 0.0, 1.0)
        _a = jax.random.uniform(jax.random.fold_in(_gk, 2), (4096, 4096)) < _pij
        _a = jnp.logical_or(_a, jnp.eye(4096, dtype=bool))
        _af = _a.astype(jnp.float32)
        _af = _af * jax.random.uniform(jax.random.fold_in(_gk, 3), (4096, 4096), jnp.float32, 0.05, 1)
        adj = _af
        return (x, adj)
    x, adj = _rec_inputs()

    def _L0_gnn_setup():
        import jax, jax.numpy as jnp
        import numpy as np
        N, D_IN, D_ATTN, STEPS, P_NUC, TAU = (2048, 256, 64, 2, 0.9, 1.0)
        LN_EPS = 1e-05

        def _xavier(key, shape):
            fan_in, fan_out = (shape[-2], shape[-1])
            lim = np.sqrt(6.0 / (fan_in + fan_out))
            return jax.random.uniform(key, shape, jnp.float32, -lim, lim)

        def _adj_from_feats(Xa, W1, W2, W3):
            Q = Xa @ W1
            K = Xa @ W3
            logits = Q @ W2 @ K.T / TAU
            idx = jnp.argsort(-logits, axis=1)
            vals = jnp.take_along_axis(logits, idx, axis=1)
            csum = jnp.cumsum(jax.nn.softmax(vals, axis=1), axis=1)
            k_i = jnp.sum(csum < P_NUC, axis=1) + 1
            ranks = jnp.arange(logits.shape[1])[None, :]
            keep_sorted = ranks < k_i[:, None]
            inv = jnp.argsort(idx, axis=1)
            keep = jnp.take_along_axis(keep_sorted, inv, axis=1)
            masked = jnp.where(keep, logits, -jnp.inf)
            return jax.nn.softmax(masked, axis=1)
        key = jax.random.key(seed)
        ks = jax.random.split(key, 9)
        return {'X': jax.random.normal(ks[0], (N, D_IN), jnp.float32), 'S': jax.random.uniform(ks[1], (N, N), jnp.float32), 'W1': _xavier(ks[2], (D_IN, D_ATTN)), 'W2': _xavier(ks[3], (D_ATTN, D_ATTN)), 'W3': _xavier(ks[4], (D_IN, D_ATTN)), 'U1': _xavier(ks[5], (STEPS, D_IN, D_IN)), 'U2': _xavier(ks[6], (STEPS, D_IN, D_IN)), 'U3': _xavier(ks[7], (STEPS, D_IN, D_IN)), 'gamma': jnp.ones((D_IN,), jnp.float32), 'beta': jnp.zeros((D_IN,), jnp.float32)}
    _L0_gnn_all = _L0_gnn_setup()
    _L0_gnn_in = {k: v for k, v in _L0_gnn_all.items() if k in ('W1', 'W2', 'W3', 'U1', 'U2', 'U3', 'gamma', 'beta')}
    del _L0_gnn_all
    return {'x': x, 'adj': adj, 'L0_gnn_W1': _L0_gnn_in['W1'], 'L0_gnn_W2': _L0_gnn_in['W2'], 'L0_gnn_W3': _L0_gnn_in['W3'], 'L0_gnn_U1': _L0_gnn_in['U1'], 'L0_gnn_U2': _L0_gnn_in['U2'], 'L0_gnn_U3': _L0_gnn_in['U3'], 'L0_gnn_gamma': _L0_gnn_in['gamma'], 'L0_gnn_beta': _L0_gnn_in['beta']}

def reference(x, adj, L0_gnn_W1, L0_gnn_W2, L0_gnn_W3, L0_gnn_U1, L0_gnn_U2, L0_gnn_U3, L0_gnn_gamma, L0_gnn_beta):
    import jax
    import jax.numpy as jnp

    def _L0_gnn_ref(X, S, W1, W2, W3, U1, U2, U3, gamma, beta):
        import jax, jax.numpy as jnp
        import numpy as np
        N, D_IN, D_ATTN, STEPS, P_NUC, TAU = (2048, 256, 64, 2, 0.9, 1.0)
        LN_EPS = 1e-05

        def _xavier(key, shape):
            fan_in, fan_out = (shape[-2], shape[-1])
            lim = np.sqrt(6.0 / (fan_in + fan_out))
            return jax.random.uniform(key, shape, jnp.float32, -lim, lim)

        def _adj_from_feats(Xa, W1, W2, W3):
            Q = Xa @ W1
            K = Xa @ W3
            logits = Q @ W2 @ K.T / TAU
            idx = jnp.argsort(-logits, axis=1)
            vals = jnp.take_along_axis(logits, idx, axis=1)
            csum = jnp.cumsum(jax.nn.softmax(vals, axis=1), axis=1)
            k_i = jnp.sum(csum < P_NUC, axis=1) + 1
            ranks = jnp.arange(logits.shape[1])[None, :]
            keep_sorted = ranks < k_i[:, None]
            inv = jnp.argsort(idx, axis=1)
            keep = jnp.take_along_axis(keep_sorted, inv, axis=1)
            masked = jnp.where(keep, logits, -jnp.inf)
            return jax.nn.softmax(masked, axis=1)
        n = X.shape[0]
        S = S + jnp.eye(n, dtype=X.dtype)
        Rf = S / jnp.clip(S.sum(axis=1, keepdims=True), 1e-12)
        Rb = S / jnp.clip(S.sum(axis=0), 1e-12)[:, None]
        Xf, Xb, Xa = (X, X, X)
        Z = jnp.zeros_like(X)
        for s in range(STEPS):
            A = _adj_from_feats(Xa, W1, W2, W3)
            Xf = Rf @ Xf
            Xb = Rb @ Xb
            Xa = A @ Xa
            Z = Z + (Xf @ U1[s] + Xb @ U2[s] + Xa @ U3[s])
        Y = X + Z
        mu = Y.mean(axis=-1, keepdims=True)
        var = Y.var(axis=-1, keepdims=True)
        return (Y - mu) / jnp.sqrt(var + LN_EPS) * gamma + beta
    h = jnp.maximum(_layernorm(x, axis=-1), 0.0)
    x = x + _L0_gnn_ref(h, adj, L0_gnn_W1, L0_gnn_W2, L0_gnn_W3, L0_gnn_U1, L0_gnn_U2, L0_gnn_U3, L0_gnn_gamma, L0_gnn_beta)
    return x

_drawn_inputs = setup_inputs


def setup_inputs(seed=0):
    import zlib

    import numpy as np

    out = dict(_drawn_inputs(seed))
    spreads = {'L0_gnn_gamma': (1.0, 0.2), 'L0_gnn_beta': (0.0, 0.1)}
    factors = {}
    for name, (base, spread) in spreads.items():
        noise = np.random.default_rng([zlib.crc32(name.encode()), seed]).standard_normal(out[name].shape)
        drawn = base * np.exp(spread * noise) if base else spread * noise
        out[name] = jnp.asarray(drawn.astype(out[name].dtype))
    for name, factor in factors.items():
        out[name] = (out[name] * factor).astype(out[name].dtype)
    return out
```

```python
import numpy as np
import concourse.bass as bass
from concourse import mybir
from contextlib import ExitStack

F32 = mybir.dt.float32
F32R = mybir.dt.float32r
BF16 = mybir.dt.bfloat16
U16 = mybir.dt.uint16
ALU = mybir.AluOpType
ACT = mybir.ActivationFunctionType
AX_X = mybir.AxisListType.X

P = 128
N = 4096
D = 256
DC = D // P
DA = 64
T = N // P
LW = 1024
LCH = N // LW
BANK = 512
TB = 4
NTB = T // TB
UB = 6 * DC // TB
SEQ_PER_TILE = (158, 173)
PIECE = 4
NPIECE = T // PIECE
RING = 4
HALF = N // 2
GROUP = 4
NGROUP = T // GROUP
P_NUC = 0.9
EPS = 1e-5
EXP_STEPS = 5
MAN_STEPS = 23
T0 = 2.0 ** -16


class Chain:

    def __init__(self, eng, sem):
        self.eng, self.sem, self.base, self.k = eng, sem, 0, 0

    def __call__(self, ins):
        ins.then_inc(self.sem, 1)
        self.k += 1
        self.eng.wait_ge(self.sem, self.base + self.k)


def build(nc, x, adj_t, W1, W2, W3, U1, U2, U3, gamma, beta, out):
    ctx = ExitStack()
    with ctx:
        def sb(name, shape, dt=F32):
            return ctx.enter_context(nc.sbuf_tensor(name, shape, dt))

        def ps(name, shape):
            return ctx.enter_context(nc.psum_tensor(name, shape, F32))

        def sem(name):
            return ctx.enter_context(nc.semaphore(name))

        h_dram = nc.dram_tensor("h_dram", [P, T, D], F32).ap()
        xa_dram = nc.dram_tensor("xa_dram", [T, P, D], F32).ap()
        q_dram = nc.dram_tensor("q_dram", [2, NGROUP, P, GROUP * P], F32).ap()

        nodes = sb("nodes", [P, T, D + 1])
        big = sb("big", [P, T, 2 * D])
        k_hi = sb("k_hi", [P, N], F32R)
        k_lo = sb("k_lo", [P, N], F32R)
        q_tile = sb("q_tile", [P, 2, P], F32R)
        probs = sb("probs", [P, 2, N])
        adj_ring = sb("adj_ring", [P, RING, PIECE, P])
        scratch = sb("scratch", [P, N], BF16)
        tied = scratch[:, 0:HALF]
        rank = scratch[:, HALF:N].bitcast(U16)
        xt = sb("xt", [P, 2, BANK])
        stage = sb("stage", [P, 6 * D])
        w3d = sb("w3d", [P, DC, P])
        w1 = sb("w1", [P, DC, DA])
        w2d = sb("w2d", [DA, P])
        t1 = stage[0:DA, 4 * D:6 * D]
        q_stack = scratch[:, 0:2 * BANK].bitcast(F32R)
        u_all = sb("u_all", [P, 6, DC, D])
        ident = sb("ident", [P, P])
        gam = sb("gam", [P, D])
        bet = sb("bet", [P, D])
        xa_out = sb("xa_out", [P, 2, D])
        h_in = xa_out[:, 0, :]
        x_in = xa_out[:, 1, :]
        y_t = sb("y_t", [P, D])
        bn = sb("bn", [P, 6])
        ln_a = sb("ln_a", [P, T])
        rinv = sb("rinv", [P, T])
        cinv = sb("cinv", [P, T])
        ln_b, ln_c = rinv, cinv
        x_stats = scratch[:, 0:12 * T].bitcast(F32).rearrange("p (t k) -> p t k", k=6)
        x_mean = scratch[:, 12 * T:14 * T].bitcast(F32)
        small = sb("small", [P, 32])
        pmax = small[:, 0:LCH]
        negmax = small[:, 4:6]
        zsum = small[:, 6:8]
        kept = small[:, 8:10]
        rkept = small[:, 10:12]
        target = small[:, 12:13]
        thr = small[:, 13:14]
        cand = small[:, 14:15]
        step = small[:, 15:16]
        mass = small[:, 16:17]
        got = small[:, 17:18]
        above = small[:, 18:19]
        limit = small[:, 19:20]
        negthr = small[:, 20:21]
        fin = small[:, 24:30]

        logits = ps("logits", [P, 2, LW])
        tr = ps("tr", [P, 2, BANK])
        acc = ps("acc", [P, 2, D])
        sx = ps("sx", [P, BANK])

        x_loaded = sem("x_loaded")
        w_loaded = sem("w_loaded")
        consts = sem("consts")
        var_ready = sem("var_ready")
        std_ready = sem("std_ready")
        affine_ready = sem("affine_ready")
        h_ready = sem("h_ready")
        h_stored = sem("h_stored")
        staged = sem("staged")
        p_tr_full = sem("p_tr_full")
        p_xt_ready = sem("p_xt_ready")
        kt_full = sem("kt_full")
        t1_ready = sem("t1_ready")
        q_full = sem("q_full")
        kq_hi = sem("kq_hi")
        kq_done = sem("kq_done")
        q_stored = sem("q_stored")
        q_loaded = [sem(f"q_loaded{b}") for b in range(2)]
        logits_full = sem("logits_full")
        logits_free = sem("logits_free")
        negmax_ready = sem("negmax_ready")
        exp_done = sem("exp_done")
        masked = sem("masked")
        tr_full = sem("tr_full")
        xt_ready = sem("xt_ready")
        xt_used = sem("xt_used")
        xa_ready = sem("xa_ready")
        xa_stored = sem("xa_stored")
        xa_back = sem("xa_back")
        adj_loaded = [sem(f"adj_loaded{s}") for s in range(RING)]
        adj_used = sem("adj_used")
        cols_added = sem("cols_added")
        sx_read = sem("sx_read")
        xb_ready = sem("xb_ready")
        cinv_ready = sem("cinv_ready")
        big_ready = sem("big_ready")
        copied = sem("copied")
        y_read = sem("y_read")
        hx_loaded = sem("hx_loaded")
        var2_ready = sem("var2_ready")
        log_done = sem("log_done")
        rstd_ready = sem("rstd_ready")
        o_ready = sem("o_ready")
        o_stored = sem("o_stored")
        dve_seq = sem("dve_seq")

        block = ctx.enter_context(nc.Block())

        def batches(t, s):
            return t * (NTB + UB) + T * NTB if s else t * NTB

        def batch_free(k):
            return k - 1 if k >= 2 else 0

        def at(t):
            return bass.ds(t, 1)

        @block.sync
        def _(sp):
            sp.dma_start(nodes[:, :, 0:D], x.rearrange("(t p) d -> p t d", p=P)).then_inc(x_loaded, 16)
            sp.dma_start(w1[:, :, :], W1.rearrange("(c p) n -> p c n", p=P)).then_inc(w_loaded, 16)
            for half in range(2):
                cols = slice(half * DA, (half + 1) * DA)
                sp.dma_start(w3d[:, :, cols], W3.rearrange("(c p) n -> p c n", p=P)).then_inc(w_loaded, 16)
                sp.dma_start(w2d[:, cols], W2).then_inc(w_loaded, 16)
            for s in range(2):
                for j, U in enumerate((U1, U2, U3)):
                    sp.dma_start(u_all[:, 3 * s + j, :, :],
                                 U[s, :, :].rearrange("(c p) n -> p c n", p=P)).then_inc(w_loaded, 16)
            sp.dma_start(gam[:, :], gamma).then_inc(w_loaded, 16)
            sp.dma_start(bet[:, :], beta).then_inc(w_loaded, 16)
            sp.wait_ge(h_ready, T)
            sp.dma_start(h_dram, nodes[:, :, 0:D]).then_inc(h_stored, 16)
            for s in range(2):
                with sp.Fori(0, NGROUP) as g:
                    sp.wait_ge(kq_done, g * 2 + (2 * NGROUP * s + 2))
                    sp.dma_start(q_dram[s, at(g), :, :], scratch[:, 0:2 * BANK].bitcast(F32)).then_inc(q_stored, 16)
                sp.wait_ge(q_stored, 16 * NGROUP * (s + 1))

                def load_q(b, g, j):
                    sp.dma_start(q_tile[:, b, :].bitcast(F32), q_dram[s, at(g), :, j * P:(j + 1) * P]).then_inc(q_loaded[b], 16)

                def load_adj(t):
                    for k in range(NPIECE):
                        n = t * NPIECE + (T * s * NPIECE + k)
                        if not isinstance(t, int) or n >= RING:
                            sp.wait_ge(adj_used, n + (1 - RING))
                            if s == 0:
                                sp.wait_ge(cols_added, n + (1 - RING))
                        sp.dma_start(adj_ring[:, k % RING, :, :],
                                     adj_t[at(t), :, k * PIECE:(k + 1) * PIECE, :]).then_inc(adj_loaded[k % RING], 16)

                def tile(t, b, g, j):
                    if not isinstance(t, int) or t > 0:
                        sp.wait_ge(logits_full, t * LCH + T * s * LCH)
                    load_q(1 - b, g, j)
                    load_adj(t)

                if s == 1:
                    sp.wait_ge(logits_full, LCH * T)
                    sp.wait_ge(cols_added, T * NPIECE)
                load_q(0, 0, 0)
                tile(0, 0, 0, 1)
                with sp.Fori(0, NGROUP - 1) as g:
                    tile(g * GROUP + 1, 1, g, 2)
                    tile(g * GROUP + 2, 0, g, 3)
                    tile(g * GROUP + 3, 1, g + 1, 0)
                    tile(g * GROUP + 4, 0, g + 1, 1)
                tile(T - 3, 1, NGROUP - 1, 2)
                tile(T - 2, 0, NGROUP - 1, 3)
                load_adj(T - 1)
                if s == 0:
                    sp.wait_ge(xa_stored, 16 * T)
                    sp.wait_ge(sx_read, T)
                    sp.wait_ge(xt_used, T * NTB)
                    sp.wait_ge(h_stored, 16)
                    sp.dma_start(nodes[:, :, 0:D], xa_dram.rearrange("t p d -> p t d")).then_inc(xa_back, 16)

        @block.gpsimd
        def _(pool):
            pool.memset(ident[:, :], 0.0).then_inc(consts, 1)
            pool.memset(nodes[:, :, D:D + 1], 1.0).then_inc(consts, 1)
            pool.memset(big[:, :, D:D + P], 0.0).then_inc(consts, 1)
            pool.wait_ge(consts, 3)
            pool.affine_select(out=ident[:, :], in_=ident[:, :], compare_op=ALU.not_equal, fill=1.0, base=0,
                               pattern=[[-1, P]], channel_multiplier=1).then_inc(consts, 1)
            for s in range(2):
                if s == 0:
                    pool.wait_ge(h_ready, T)
                else:
                    pool.wait_ge(xa_back, 16)
                with pool.Fori(0, NGROUP) as g:
                    pool.tensor_copy(stage[:, 0:GROUP * D].rearrange("p (j d) -> p j d", d=D),
                                     nodes[:, bass.ds(g * GROUP, GROUP), 0:D]).then_inc(staged, 1)
                    pool.wait_ge(p_tr_full, g * 2 + (2 * NGROUP * s + 2))
                if s == 0:
                    with pool.Fori(0, T) as t:
                        for k in range(NPIECE):
                            pool.wait_ge(adj_loaded[k % RING], t * (16 * NPIECE // RING) + 16 * (k // RING + 1))
                            cols = big[:, k * PIECE:(k + 1) * PIECE, D:D + P]
                            pool.tensor_tensor(out=cols, in0=cols, in1=adj_ring[:, k % RING, :, :],
                                               op=ALU.add).then_inc(cols_added, 1)
                            pool.wait_ge(cols_added, t * NPIECE + (k + 1))
                else:
                    def rows(t):
                        pool.tensor_copy(stage[:, 0:2 * D].rearrange("p (a d) -> p a d", a=1), big[:, at(t), :]).then_inc(copied, 1)
                        pool.tensor_copy(stage[:, 2 * D:3 * D].rearrange("p (a d) -> p a d", a=1), nodes[:, at(t), 0:D]).then_inc(copied, 1)

                    def load_hx(t):
                        pool.dma_start(h_in.rearrange("p (a d) -> p a d", a=1), h_dram[:, at(t), :]).then_inc(hx_loaded, 16)
                        pool.dma_start(x_in, x[bass.ds(t * P, P), :]).then_inc(hx_loaded, 16)

                    pool.wait_ge(big_ready, T)
                    rows(0)
                    load_hx(0)
                    with pool.Fori(1, T) as t:
                        pool.wait_ge(xt_used, batches(t, s))
                        rows(t)
                        pool.wait_ge(o_ready, t)
                        pool.dma_start(out[bass.ds(t * P - P, P), :], x_in).then_inc(o_stored, 16)
                        pool.wait_ge(o_stored, t * 16)
                        load_hx(t)
            pool.wait_ge(o_ready, T)
            pool.dma_start(out[(T - 1) * P:T * P, :], x_in).then_inc(o_stored, 16)
            pool.wait_ge(o_stored, 16 * T)

        @block.scalar
        def _(act):
            act.wait_ge(var_ready, 1)
            nc.scalar.activation(ln_b[:, :], ln_a[:, :], ACT.Sqrt).then_inc(std_ready, 1)
            act.wait_ge(affine_ready, 1)
            with act.Fori(0, T) as t:
                row = nodes[:, at(t), 0:D]
                act.activation(row, row, ACT.Relu, bias=ln_b[:, at(t)], scale=ln_a[:, at(t)]).then_inc(h_ready, 1)
            for s in range(2):
                with act.Fori(0, NGROUP) as g:
                    for c in range(DC):
                        act.wait_ge(p_tr_full, g * 2 + (2 * NGROUP * s + c + 1))
                        act.activation(xt[:, c, :], tr[:, c, :], ACT.Copy).then_inc(p_xt_ready, 1)
                    act.wait_ge(kt_full, g + (NGROUP * s + 1))
                    act.activation(t1, logits[0:DA, 0, BANK:2 * BANK], ACT.Copy).then_inc(t1_ready, 1)
                    act.activation(k_hi[:, bass.ds(g * BANK, BANK)], logits[:, 0, 0:BANK], ACT.Copy).then_inc(kq_hi, 1)
                    act.wait_ge(q_full, g + (NGROUP * s + 1))
                    act.activation(q_stack, logits[:, 1, 0:BANK], ACT.Copy).then_inc(kq_hi, 1)
                    act.wait_ge(q_stored, g * 16 + (NGROUP * s + 1) * 16)

                def exps(t, b):
                    act.wait_ge(negmax_ready, t + (T * s + 1))
                    act.activation(probs[:, b, :], probs[:, b, :], ACT.Exp, bias=negmax[:, b:b + 1],
                                   accum_out=zsum[:, b:b + 1]).then_inc(exp_done, 1)

                def to_sbuf(t, k):
                    act.wait_ge(tr_full, batches(t, s) + (k + 1))
                    act.wait_ge(xt_used, batches(t, s) + batch_free(k))
                    act.activation(xt[:, k % 2, :], tr[:, k % 2, :], ACT.Copy).then_inc(xt_ready, 1)

                def inverse_std(t):
                    act.wait_ge(var2_ready, t + 1)
                    act.activation(fin[:, 1:2], fin[:, 0:1], ACT.Ln).then_inc(log_done, 1)
                    act.wait_ge(log_done, t + 1)
                    act.activation(fin[:, 2:3], fin[:, 1:2], ACT.Exp, scale=-0.5).then_inc(rstd_ready, 1)

                def tile(t, b, last=False):
                    if not last:
                        exps(t + 1, 1 - b)
                    if s and not (isinstance(t, int) and t == 0):
                        inverse_std(t - 1)
                    for k in range(NTB):
                        to_sbuf(t, k)
                    act.wait_ge(xt_used, batches(t, s) + NTB)
                    if s == 0:
                        act.wait_ge(xa_stored, t * 16)
                        act.activation(xa_out[:, b, :], acc[:, 0, :], ACT.Copy,
                                       scale=rkept[:, b:b + 1]).then_inc(xa_ready, 1)
                        act.wait_ge(xa_ready, t + 1)
                        act.dma_start(xa_dram[at(t), :, :], xa_out[:, b, :]).then_inc(xa_stored, 16)
                    else:
                        act.activation(stage[:, 5 * D:6 * D], acc[:, 0, :], ACT.Copy,
                                       scale=rkept[:, b:b + 1]).then_inc(xa_ready, 1)
                        for k in range(NTB, NTB + UB):
                            to_sbuf(t, k)

                exps(0, 0)
                tile(0, 0)
                with act.Fori(0, T // 2 - 1) as i:
                    tile(i * 2 + 1, 1)
                    tile(i * 2 + 2, 0)
                tile(T - 1, 1, last=True)
                if s == 0:
                    act.wait_ge(cinv_ready, 1)
                    with act.Fori(0, T) as t:
                        act.activation(big[:, at(t), D:2 * D], big[:, at(t), 0:D], ACT.Copy,
                                       scale=cinv[:, at(t)]).then_inc(xb_ready, 1)
                else:
                    inverse_std(T - 1)

        @block.tensor
        def _(pe):
            pe.wait_ge(w_loaded, 16 * 13)
            pe.wait_ge(consts, 4)
            for s in range(2):
                with pe.Fori(0, NGROUP) as g:
                    pe.wait_ge(staged, g + (NGROUP * s + 1))
                    for c in range(DC):
                        for j in range(GROUP):
                            ins = nc.tensor.transpose(tr[:, c, j * P:(j + 1) * P],
                                                      stage[:, j * D + c * P:j * D + (c + 1) * P], ident[:, :])
                        ins.then_inc(p_tr_full, 1)
                    pe.wait_ge(p_xt_ready, g * 2 + (NGROUP * s * 2 + 2))
                    for c in range(DC):
                        nc.tensor.matmul(logits[:, 0, 0:BANK], w3d[:, c, :], xt[:, c, :], start=c == 0, stop=c == DC - 1)
                    for c in range(DC):
                        ins = nc.tensor.matmul(logits[0:DA, 0, BANK:2 * BANK], w1[:, c, :], xt[:, c, :],
                                               start=c == 0, stop=c == DC - 1)
                    ins.then_inc(kt_full, 1)
                    pe.wait_ge(t1_ready, g + (NGROUP * s + 1))
                    nc.tensor.matmul(logits[:, 1, 0:BANK], w2d[:, :], t1, start=True, stop=True).then_inc(q_full, 1)
                    pe.wait_ge(kq_done, g * 2 + (NGROUP * s * 2 + 2))
                if s == 1:
                    pe.wait_ge(big_ready, T)

                def logit_rows(t, b, loads):
                    pe.wait_ge(q_loaded[b], loads * 16 + T // 2 * s * 16)
                    for k in range(LCH):
                        n = t * LCH + (T * s * LCH + k)
                        if not isinstance(t, int) or n >= 2:
                            pe.wait_ge(logits_free, n - 1)
                        for j in range(LW // BANK):
                            cols = slice(k * LW + j * BANK, k * LW + (j + 1) * BANK)
                            o = logits[:, k % 2, j * BANK:(j + 1) * BANK]
                            nc.tensor.matmul(o, q_tile[:, b, :], k_hi[:, cols], start=True, stop=False)
                            ins = nc.tensor.matmul(o, q_tile[:, b, :], k_lo[:, cols], start=False, stop=True)
                        ins.then_inc(logits_full, 1)

                def adj_rows(t):
                    pe.wait_ge(sx_read, t + T * s)
                    width = D + 1 if s == 0 else 2 * D
                    src = nodes if s == 0 else big
                    for k in range(NPIECE):
                        pe.wait_ge(adj_loaded[k % RING],
                                   t * (16 * NPIECE // RING) + (T * s * NPIECE // RING + k // RING + 1) * 16)
                        for c in range(PIECE):
                            ch = k * PIECE + c
                            ins = nc.tensor.matmul(sx[:, 0:width], adj_ring[:, k % RING, c, :], src[:, ch, 0:width],
                                                   start=ch == 0, stop=ch == T - 1)
                        ins.then_inc(adj_used, 1)

                def batch(t, k, block_of):
                    pe.wait_ge(xt_ready, batches(t, s) + batch_free(k))
                    for j in range(TB):
                        ins = nc.tensor.transpose(tr[:, k % 2, j * P:(j + 1) * P], block_of(k, j), ident[:, :])
                    ins.then_inc(tr_full, 1)

                def attend(t, b):
                    def block_of(k, j):
                        return probs[:, b, (k * TB + j) * P:(k * TB + j + 1) * P]

                    pe.wait_ge(masked, t + (T * s + 1))
                    batch(t, 0, block_of)
                    pe.wait_ge(xa_ready, t + T * s)
                    for k in range(NTB):
                        if k + 1 < NTB:
                            batch(t, k + 1, block_of)
                        pe.wait_ge(xt_ready, batches(t, s) + (k + 1))
                        for j in range(TB):
                            ch = k * TB + j
                            ins = nc.tensor.matmul(acc[:, 0, :], xt[:, k % 2, j * P:(j + 1) * P], nodes[:, ch, 0:D],
                                                   start=ch == 0, stop=ch == T - 1)
                        ins.then_inc(xt_used, 1)

                def u_products(t):
                    def block_of(k, j):
                        n = (k - NTB) * TB + j
                        return stage[:, n * P:(n + 1) * P]

                    pe.wait_ge(copied, t * 2 + 2)
                    pe.wait_ge(sx_read, t + (T + 1))
                    pe.wait_ge(xa_ready, t + (T + 1))
                    pe.wait_ge(y_read, t)
                    batch(t, NTB, block_of)
                    for k in range(NTB, NTB + UB):
                        if k + 1 < NTB + UB:
                            batch(t, k + 1, block_of)
                        pe.wait_ge(xt_ready, batches(t, s) + (k + 1))
                        for j in range(TB):
                            n = (k - NTB) * TB + j
                            ins = nc.tensor.matmul(acc[:, 1, :], xt[:, k % 2, j * P:(j + 1) * P],
                                                   u_all[:, n // DC, n % DC, :], start=n == 0, stop=n == UB * TB - 1)
                        ins.then_inc(xt_used, 1)

                def tile(t, b, last=False, loads=None):
                    if not last:
                        logit_rows(t + 1, 1 - b, loads)
                    adj_rows(t)
                    attend(t, b)
                    if s:
                        u_products(t)

                logit_rows(0, 0, 1)
                tile(0, 0, loads=1)
                with pe.Fori(0, T // 2 - 1) as i:
                    tile(i * 2 + 1, 1, loads=i + 2)
                    tile(i * 2 + 2, 0, loads=i + 2)
                tile(T - 1, 1, last=True)

        @block.vector
        def _(dve):
            v = nc.vector
            seq = Chain(dve, dve_seq)

            def variance(mean, var, half, stat):
                seq(v.tensor_tensor(mean, stat(1), stat(4), ALU.add))
                seq(v.tensor_scalar(mean, mean, 0.5, None, ALU.mult))
                seq(v.tensor_tensor(half, mean, stat(1), ALU.subtract))
                seq(v.tensor_tensor(half, half, half, ALU.mult))
                seq(v.tensor_tensor(var, stat(2), stat(5), ALU.add))
                seq(v.tensor_scalar(var, var, 1.0 / D, None, ALU.mult))
                seq(v.tensor_tensor(var, var, half, ALU.add))

            dve.wait_ge(x_loaded, 16)
            with dve.Fori(0, T) as t:
                v.bn_stats(x_stats[:, at(t), :].rearrange("p a d -> p (a d)"),
                           nodes[:, at(t), 0:D].rearrange("p a d -> p (a d)")).then_inc(dve_seq, 1)
            seq.base, seq.k = T, 0
            dve.wait_ge(dve_seq, T)
            variance(x_mean, ln_a[:, :], ln_b[:, :], lambda k: x_stats[:, :, k])
            v.tensor_scalar(ln_a[:, :], ln_a[:, :], EPS, None, ALU.add).then_inc(var_ready, 1)
            dve.wait_ge(std_ready, 1)
            seq(v.reciprocal(ln_c[:, :], ln_b[:, :]))
            seq(v.tensor_tensor(ln_b[:, :], ln_c[:, :], ln_c[:, :], ALU.mult))
            seq(v.tensor_tensor(ln_b[:, :], ln_b[:, :], ln_a[:, :], ALU.mult))
            seq(v.tensor_scalar(ln_b[:, :], ln_b[:, :], -0.5, 1.5, ALU.mult, ALU.add))
            seq(v.tensor_tensor(ln_a[:, :], ln_c[:, :], ln_b[:, :], ALU.mult))
            seq(v.tensor_tensor(ln_b[:, :], x_mean, ln_a[:, :], ALU.mult))
            v.tensor_scalar(ln_b[:, :], ln_b[:, :], -1.0, None, ALU.mult).then_inc(affine_ready, 1)

            for s in range(2):
                with dve.Fori(0, NGROUP) as g:
                    kcols = bass.ds(g * BANK, BANK)
                    dve.wait_ge(kq_hi, g * 2 + (NGROUP * s * 2 + 1))
                    v.tensor_tensor(k_lo[:, kcols], logits[:, 0, 0:BANK], k_hi[:, kcols].bitcast(F32),
                                    ALU.subtract).then_inc(kq_done, 1)
                    dve.wait_ge(kq_hi, g * 2 + (NGROUP * s * 2 + 2))
                    v.tensor_tensor(scratch[DA:P, 0:2 * BANK].bitcast(F32R), logits[DA:P, 1, 0:BANK], scratch[DA:P, 0:2 * BANK].bitcast(F32),
                                    ALU.subtract).then_inc(kq_done, 1)

                def evacuate(t, b):
                    for k in range(LCH):
                        dve.wait_ge(logits_full, t * LCH + (T * s * LCH + k + 1))
                        v.tensor_scalar(probs[:, b, k * LW:(k + 1) * LW], logits[:, k % 2, :], 1.0, None, ALU.mult,
                                        ALU.max, accum_out=pmax[:, k:k + 1]).then_inc(logits_free, 1)
                    dve.wait_ge(logits_free, t * LCH + (T * s + 1) * LCH)
                    seq(v.reduce_max(negmax[:, b:b + 1], pmax[:, :], AX_X))
                    v.tensor_scalar(negmax[:, b:b + 1], negmax[:, b:b + 1], -1.0, None, ALU.mult)\
                        .then_inc(negmax_ready, 1)

                def mass_at(b, value, op):
                    seq(v.scalar_tensor_tensor(out=scratch[:, :], in0=probs[:, b, :], scalar=value[:, :],
                                               in1=probs[:, b, :], op0=op, op1=ALU.mult, accum_out=mass[:, :]))

                def raise_threshold(b):
                    mass_at(b, cand, ALU.is_ge)
                    seq(v.tensor_scalar(got[:, :], mass[:, :], target[:, :], cand[:, :], ALU.is_ge, ALU.mult))
                    seq(v.tensor_scalar(thr[:, :], got[:, :], thr[:, :], None, ALU.max))

                def finish(t):
                    dve.wait_ge(xt_used, batches(t + 1, 1))
                    dve.wait_ge(hx_loaded, (t + 1) * 32)
                    v.tensor_tensor(y_t[:, :], acc[:, 1, :], h_in, ALU.add).then_inc(y_read, 1)
                    dve.wait_ge(y_read, t + 1)
                    seq(v.bn_stats(bn[:, :], y_t[:, :]))
                    variance(fin[:, 4:5], fin[:, 5:6], fin[:, 3:4], lambda k: bn[:, k:k + 1])
                    v.tensor_scalar(fin[:, 0:1], fin[:, 5:6], EPS, None, ALU.add).then_inc(var2_ready, 1)
                    dve.wait_ge(rstd_ready, t + 1)
                    seq(v.tensor_scalar(fin[:, 3:4], fin[:, 2:3], fin[:, 2:3], fin[:, 0:1], ALU.mult, ALU.mult))
                    seq(v.tensor_scalar(fin[:, 3:4], fin[:, 3:4], -0.5, 1.5, ALU.mult, ALU.add))
                    seq(v.tensor_scalar(fin[:, 3:4], fin[:, 3:4], fin[:, 2:3], None, ALU.mult))
                    seq(v.tensor_scalar(y_t[:, :], y_t[:, :], fin[:, 4:5], fin[:, 3:4], ALU.subtract, ALU.mult))
                    seq(v.tensor_tensor(y_t[:, :], y_t[:, :], gam[:, :], ALU.mult))
                    seq(v.tensor_tensor(y_t[:, :], y_t[:, :], bet[:, :], ALU.add))
                    v.tensor_tensor(x_in, y_t[:, :], x_in, ALU.add).then_inc(o_ready, 1)

                def search_exponent(b):
                    seq(v.tensor_scalar(target[:, :], zsum[:, b:b + 1], P_NUC, None, ALU.mult))
                    seq(v.memset(thr[:, :], T0))
                    for e in reversed(range(EXP_STEPS)):
                        seq(v.tensor_scalar(cand[:, :], thr[:, :], 2.0 ** 2 ** e, None, ALU.mult))
                        raise_threshold(b)
                    seq(v.tensor_scalar(step[:, :], thr[:, :], 0.5, None, ALU.mult))

                def search_mantissa(b):
                    base, k = seq.base, seq.k
                    with dve.Fori(0, MAN_STEPS) as j:
                        seq.base, seq.k = j * 5 + (base + k), 0
                        seq(v.tensor_scalar(cand[:, :], thr[:, :], step[:, :], None, ALU.add))
                        raise_threshold(b)
                        seq(v.tensor_scalar(step[:, :], step[:, :], 0.5, None, ALU.mult))
                        assert seq.k == 5
                    seq.base, seq.k = base, k + 5 * MAN_STEPS

                def read_adj_product(t, first):
                    dve.wait_ge(adj_used, (t + 1) * NPIECE + T * s * NPIECE)
                    if s == 0:
                        seq(v.tensor_tensor(big[:, at(t), 0:D].rearrange("p a d -> p (a d)"), sx[:, 0:D],
                                            nodes[:, at(t), 0:D].rearrange("p a d -> p (a d)"), ALU.add))
                        v.tensor_scalar(rinv[:, at(t)], sx[:, D:D + 1], 1.0, 1e-12, ALU.add, ALU.max)\
                            .then_inc(sx_read, 1)
                        return
                    if not first:
                        dve.wait_ge(xt_used, batches(t, s))
                    seq(v.tensor_tensor(stage[:, 3 * D:5 * D], sx[:, :],
                                        big[:, at(t), :].rearrange("p a d -> p (a d)"), ALU.add))
                    seq(v.tensor_scalar(stage[:, 3 * D:4 * D], stage[:, 3 * D:4 * D], rinv[:, at(t)], None, ALU.mult))
                    v.tensor_scalar(stage[:, 4 * D:5 * D], stage[:, 4 * D:5 * D], cinv[:, at(t)], None, ALU.mult)\
                        .then_inc(sx_read, 1)

                def mask(t, b):
                    mass_at(b, thr, ALU.is_gt)
                    seq(v.tensor_scalar(above[:, :], target[:, :], mass[:, :], None, ALU.subtract))
                    seq(v.reciprocal(limit[:, :], thr[:, :]))
                    seq(v.tensor_scalar(limit[:, :], above[:, :], limit[:, :], 1.0, ALU.mult, ALU.add))
                    seq(v.tensor_scalar(limit[:, :], limit[:, :], 1.5, None, ALU.max))
                    seq(v.tensor_scalar(negthr[:, :], thr[:, :], -1.0, None, ALU.mult))
                    for hh in range(2):
                        cols = probs[:, b, hh * HALF:(hh + 1) * HALF]
                        if hh:
                            seq(v.tensor_copy(got[:, :], rank[:, HALF - 1:HALF]))
                        seq(v.tensor_scalar(tied, cols, thr[:, :], None, ALU.is_equal))
                        seq(v.tensor_tensor_scan(rank, tied, tied, got[:, :] if hh else 0.0, ALU.add, ALU.max))
                        seq(v.scalar_tensor_tensor(out=tied, in0=rank, scalar=limit[:, :], in1=tied,
                                                   op0=ALU.is_ge, op1=ALU.mult))
                        seq(v.scalar_tensor_tensor(out=cols, in0=cols, scalar=thr[:, :], in1=cols,
                                                   op0=ALU.is_ge, op1=ALU.mult))
                        seq(v.scalar_tensor_tensor(out=cols, in0=tied, scalar=negthr[:, :], in1=cols,
                                                   op0=ALU.mult, op1=ALU.add, accum_out=kept[:, hh:hh + 1]))
                    seq(v.tensor_tensor(got[:, :], kept[:, 0:1], kept[:, 1:2], ALU.add))
                    v.reciprocal(rkept[:, b:b + 1], got[:, :]).then_inc(masked, 1)

                def tile(t, b, first=False, last=False):
                    dve.wait_ge(exp_done, t + (T * s + 1))
                    search_exponent(b)
                    if not last:
                        if not first:
                            dve.wait_ge(tr_full, batches(t, s) - (UB if s else 0))
                        evacuate(t + 1, 1 - b)
                    search_mantissa(b)
                    read_adj_product(t, first)
                    if s and not first:
                        finish(t - 1)
                    mask(t, b)

                evacuate(0, 0)
                tile(0, 0, first=True)
                seq.base, seq.k = seq.base + seq.k, 0
                base = seq.base
                per = SEQ_PER_TILE[s]
                with dve.Fori(0, T // 2 - 1) as i:
                    seq.base, seq.k = i * (2 * per) + base, 0
                    tile(i * 2 + 1, 1)
                    assert seq.k == per, seq.k
                    tile(i * 2 + 2, 0)
                seq.base, seq.k = base + (T - 2) * per, 0
                tile(T - 1, 1, last=True)
                if s == 0:
                    dve.wait_ge(cols_added, T * NPIECE)
                    seq(v.reduce_sum(cinv[:, :], big[:, :, D:D + P], AX_X))
                    seq(v.tensor_scalar(cinv[:, :], cinv[:, :], 1.0, 1e-12, ALU.add, ALU.max))
                    seq(v.reciprocal(rinv[:, :], rinv[:, :]))
                    v.reciprocal(cinv[:, :], cinv[:, :]).then_inc(cinv_ready, 1)
                    with dve.Fori(0, T) as t:
                        dve.wait_ge(xb_ready, t + 1)
                        v.tensor_scalar(big[:, at(t), 0:D], big[:, at(t), 0:D], rinv[:, at(t)], None, ALU.mult)\
                            .then_inc(big_ready, 1)
                else:
                    finish(T - 1)


def kernel(x, adj, L0_gnn_W1, L0_gnn_W2, L0_gnn_W3, L0_gnn_U1, L0_gnn_U2, L0_gnn_U3, L0_gnn_gamma, L0_gnn_beta):
    import concourse.bacc as bacc
    from concourse.bass_utils import run_bass_kernel_spmd

    def arr(a):
        return np.ascontiguousarray(np.asarray(a))

    arrays = {
        "x_in_dram": arr(x),
        "adj_t_dram": arr(np.asarray(adj).reshape(T, P, T, P).transpose(0, 3, 2, 1)),
        "w1_dram": arr(L0_gnn_W1), "w2_dram": arr(L0_gnn_W2), "w3_dram": arr(L0_gnn_W3),
        "u1_dram": arr(L0_gnn_U1), "u2_dram": arr(L0_gnn_U2), "u3_dram": arr(L0_gnn_U3),
        "gamma_dram": arr(np.broadcast_to(np.asarray(L0_gnn_gamma), (P, D))),
        "beta_dram": arr(np.broadcast_to(np.asarray(L0_gnn_beta), (P, D))),
    }
    nc = bacc.Bacc("TRN2", target_bir_lowering=False, num_devices=1)
    args = [nc.dram_tensor(n, a.shape, mybir.dt.from_np(a.dtype), kind="ExternalInput").ap()
            for n, a in arrays.items()]
    out = nc.dram_tensor("out_dram", (N, D), F32, kind="ExternalOutput").ap()
    build(nc, *args, out)
    r = run_bass_kernel_spmd(nc, [arrays], core_ids=[0])
    return r.results[0]["out_dram"]
```

```python
import numpy as np
import concourse.bass as bass
from concourse import mybir
from contextlib import ExitStack

F32 = mybir.dt.float32
F32R = mybir.dt.float32r
BF16 = mybir.dt.bfloat16
U16 = mybir.dt.uint16
U32 = mybir.dt.uint32
ALU = mybir.AluOpType
ACT = mybir.ActivationFunctionType
AX_X = mybir.AxisListType.X

P = 128
N = 4096
D = 256
DC = D // P
DA = 64
T = N // P
LW = 1024
LCH = N // LW
BANK = 512
TB = 4
NTB = T // TB
UB = 6 * DC // TB
SEQ_PER_PASS = 8
ROOM = 0.05
SEQ_PER_TILE = (64, 101)
PIECE = 4
NPIECE = T // PIECE
RING = 4
GROUP = 4
NGROUP = T // GROUP
P_NUC = 0.9
EPS = 1e-5
FIRST = 0.01
AIM = 3.0
FADE = 0.7
EDGE = 0.02
PASSES = (6, 8)
ROUND_PASSES = 4
ROUNDS = 44


class Chain:

    def __init__(self, eng, sem):
        self.eng, self.sem, self.base, self.k = eng, sem, 0, 0

    def __call__(self, ins):
        ins.then_inc(self.sem, 1)
        self.k += 1
        self.eng.wait_ge(self.sem, self.base + self.k)


def build(nc, x, adj_t, W1, W2, W3, U1, U2, U3, gamma, beta, out):
    ctx = ExitStack()
    with ctx:
        def sb(name, shape, dt=F32):
            return ctx.enter_context(nc.sbuf_tensor(name, shape, dt))

        def ps(name, shape):
            return ctx.enter_context(nc.psum_tensor(name, shape, F32))

        def sem(name):
            return ctx.enter_context(nc.semaphore(name))

        h_dram = nc.dram_tensor("h_dram", [P, T, D], F32).ap()
        xa_dram = nc.dram_tensor("xa_dram", [T, P, D], F32).ap()
        q_dram = nc.dram_tensor("q_dram", [2, NGROUP, P, 2, GROUP * P], F32).ap()

        nodes = sb("nodes", [P, T, D + 1])
        big = sb("big", [P, T, 2 * D])
        k_stack = sb("k_stack", [P, N], F32R)
        q_tile = sb("q_tile", [P, 2, 2, P], F32R)
        probs = sb("probs", [P, 2, N])
        adj_ring = sb("adj_ring", [P, RING, PIECE, P])
        scratch = sb("scratch", [P, N])
        tied = scratch[:, 0:N // 2].bitcast(BF16)
        rank = scratch[:, N // 2:N].bitcast(U16)
        xt = sb("xt", [P, 2, BANK])
        stage = sb("stage", [P, 6 * D])
        w3d = sb("w3d", [P, DC, P])
        w1 = sb("w1", [P, DC, DA])
        w2d = sb("w2d", [DA, P])
        t1 = stage[0:DA, 4 * D:6 * D]
        q_parts = scratch[:, 0:2 * BANK]
        u_all = sb("u_all", [P, 6, DC, D])
        ident = sb("ident", [P, P])
        gam = sb("gam", [P, D])
        bet = sb("bet", [P, D])
        xa_out = sb("xa_out", [P, 2, D])
        h_in = xa_out[:, 0, :]
        x_in = xa_out[:, 1, :]
        y_t = sb("y_t", [P, D])
        bn = sb("bn", [P, 6])
        ln_a = sb("ln_a", [P, T])
        rinv = sb("rinv", [P, T])
        cinv = sb("cinv", [P, T])
        ln_b, ln_c = rinv, cinv
        x_stats = scratch[:, 0:6 * T].rearrange("p (t k) -> p t k", k=6)
        x_mean = scratch[:, 6 * T:7 * T]
        small = sb("small", [P, 32])
        pmax = small[:, 0:LCH]
        negmax = small[:, 4:6]
        zsum = small[:, 6:8]
        rkept = small[:, 8:10]
        target = small[:, 12:13]
        thr = small[:, 13:14]
        negthr = small[:, 14:15]
        above = small[:, 15:16]
        limit = small[:, 16:17]
        kept = small[:, 17:18]
        numer = small[:, 18:19]
        ratio = small[:, 19:20]
        gap = small[:, 20:22]
        fin = small[:, 24:30]
        lo = sb("lo", [P, 3])
        hi = sb("hi", [P, 3])
        new = sb("new", [P, 3])
        reaches = sb("reaches", [P, 3], U32)
        misses = sb("misses", [P, 3], U32)
        best = sb("best", [P, 9])
        best_sum = sb("best_sum", [P, 8])
        best_ok = sb("best_ok", [P, 9])
        flag = sb("flag", [P, 32])
        flag_t = sb("flag_t", [P, 32])
        pad = sb("pad", [P, 2])
        flag_q = sb("flag_q", [P, 4])
        flag_i = sb("flag_i", [P, 1], mybir.dt.int32)

        logits = ps("logits", [P, 2, LW])
        tr = ps("tr", [P, 2, BANK])
        acc = ps("acc", [P, 2, D])
        sx = ps("sx", [P, BANK])

        x_loaded = sem("x_loaded")
        w_loaded = sem("w_loaded")
        consts = sem("consts")
        var_ready = sem("var_ready")
        std_ready = sem("std_ready")
        affine_ready = sem("affine_ready")
        h_ready = sem("h_ready")
        h_stored = sem("h_stored")
        staged = sem("staged")
        p_tr_full = sem("p_tr_full")
        p_xt_ready = sem("p_xt_ready")
        kt_full = sem("kt_full")
        t1_ready = sem("t1_ready")
        q_full = sem("q_full")
        kq_hi = sem("kq_hi")
        kq_done = sem("kq_done")
        q_stored = sem("q_stored")
        q_loaded = [sem(f"q_loaded{b}") for b in range(2)]
        logits_full = sem("logits_full")
        logits_free = sem("logits_free")
        negmax_ready = sem("negmax_ready")
        exp_done = sem("exp_done")
        masked = sem("masked")
        tr_full = sem("tr_full")
        xt_ready = sem("xt_ready")
        xt_used = sem("xt_used")
        xa_ready = sem("xa_ready")
        xa_stored = sem("xa_stored")
        xa_back = sem("xa_back")
        adj_loaded = [sem(f"adj_loaded{s}") for s in range(RING)]
        adj_used = sem("adj_used")
        cols_added = sem("cols_added")
        sx_read = sem("sx_read")
        xb_ready = sem("xb_ready")
        cinv_ready = sem("cinv_ready")
        big_ready = sem("big_ready")
        copied = sem("copied")
        y_read = sem("y_read")
        hx_loaded = sem("hx_loaded")
        var2_ready = sem("var2_ready")
        log_done = sem("log_done")
        rstd_ready = sem("rstd_ready")
        o_ready = sem("o_ready")
        o_stored = sem("o_stored")
        dve_seq = sem("dve_seq")
        tie_seq = sem("tie_seq")
        round_seq = sem("round_seq")

        block = ctx.enter_context(nc.Block())

        def batches(t, s):
            return t * (NTB + UB) + T * NTB if s else t * NTB

        def batch_free(k):
            return k - 1 if k >= 2 else 0

        def at(t):
            return bass.ds(t, 1)

        @block.sync
        def _(sp):
            sp.dma_start(nodes[:, :, 0:D], x.rearrange("(t p) d -> p t d", p=P)).then_inc(x_loaded, 16)
            sp.dma_start(w1[:, :, :], W1.rearrange("(c p) n -> p c n", p=P)).then_inc(w_loaded, 16)
            for half in range(2):
                cols = slice(half * DA, (half + 1) * DA)
                sp.dma_start(w3d[:, :, cols], W3.rearrange("(c p) n -> p c n", p=P)).then_inc(w_loaded, 16)
                sp.dma_start(w2d[:, cols], W2).then_inc(w_loaded, 16)
            for s in range(2):
                for j, U in enumerate((U1, U2, U3)):
                    sp.dma_start(u_all[:, 3 * s + j, :, :],
                                 U[s, :, :].rearrange("(c p) n -> p c n", p=P)).then_inc(w_loaded, 16)
            sp.dma_start(gam[:, :], gamma).then_inc(w_loaded, 16)
            sp.dma_start(bet[:, :], beta).then_inc(w_loaded, 16)
            sp.wait_ge(h_ready, T)
            sp.dma_start(h_dram, nodes[:, :, 0:D]).then_inc(h_stored, 16)
            for s in range(2):
                with sp.Fori(0, NGROUP) as g:
                    sp.wait_ge(kq_done, g * 2 + (2 * NGROUP * s + 2))
                    sp.dma_start(q_dram[s, at(g), :, :, :], q_parts.rearrange("p (h n) -> p h n", h=2)).then_inc(q_stored, 16)
                sp.wait_ge(q_stored, 16 * NGROUP * (s + 1))

                def load_q(b, g, j):
                    sp.dma_start(q_tile[:, b, :, :].bitcast(F32), q_dram[s, at(g), :, :, j * P:(j + 1) * P]).then_inc(q_loaded[b], 16)

                def load_adj(t):
                    for k in range(NPIECE):
                        n = t * NPIECE + (T * s * NPIECE + k)
                        if not isinstance(t, int) or n >= RING:
                            sp.wait_ge(adj_used, n + (1 - RING))
                            if s == 0:
                                sp.wait_ge(cols_added, n + (1 - RING))
                        sp.dma_start(adj_ring[:, k % RING, :, :],
                                     adj_t[at(t), :, k * PIECE:(k + 1) * PIECE, :]).then_inc(adj_loaded[k % RING], 16)

                def tile(t, b, g, j):
                    if not isinstance(t, int) or t > 0:
                        sp.wait_ge(logits_full, t * LCH + T * s * LCH)
                    load_q(1 - b, g, j)
                    load_adj(t)

                if s == 1:
                    sp.wait_ge(logits_full, LCH * T)
                    sp.wait_ge(cols_added, T * NPIECE)
                load_q(0, 0, 0)
                tile(0, 0, 0, 1)
                with sp.Fori(0, NGROUP - 1) as g:
                    tile(g * GROUP + 1, 1, g, 2)
                    tile(g * GROUP + 2, 0, g, 3)
                    tile(g * GROUP + 3, 1, g + 1, 0)
                    tile(g * GROUP + 4, 0, g + 1, 1)
                tile(T - 3, 1, NGROUP - 1, 2)
                tile(T - 2, 0, NGROUP - 1, 3)
                load_adj(T - 1)
                if s == 0:
                    sp.wait_ge(xa_stored, 16 * T)
                    sp.wait_ge(sx_read, T)
                    sp.wait_ge(xt_used, T * NTB)
                    sp.wait_ge(h_stored, 16)
                    sp.dma_start(nodes[:, :, 0:D], xa_dram.rearrange("t p d -> p t d")).then_inc(xa_back, 16)

        @block.gpsimd
        def _(pool):
            pool.memset(ident[:, :], 0.0).then_inc(consts, 1)
            pool.memset(nodes[:, :, D:D + 1], 1.0).then_inc(consts, 1)
            pool.memset(big[:, :, D:D + P], 0.0).then_inc(consts, 1)
            pool.wait_ge(consts, 3)
            pool.affine_select(out=ident[:, :], in_=ident[:, :], compare_op=ALU.not_equal, fill=1.0, base=0,
                               pattern=[[-1, P]], channel_multiplier=1).then_inc(consts, 1)
            for s in range(2):
                if s == 0:
                    pool.wait_ge(h_ready, T)
                else:
                    pool.wait_ge(xa_back, 16)
                with pool.Fori(0, NGROUP) as g:
                    pool.tensor_copy(stage[:, 0:GROUP * D].rearrange("p (j d) -> p j d", d=D),
                                     nodes[:, bass.ds(g * GROUP, GROUP), 0:D]).then_inc(staged, 1)
                    pool.wait_ge(p_tr_full, g * 2 + (2 * NGROUP * s + 2))
                if s == 0:
                    with pool.Fori(0, T) as t:
                        for k in range(NPIECE):
                            pool.wait_ge(adj_loaded[k % RING], t * (16 * NPIECE // RING) + 16 * (k // RING + 1))
                            cols = big[:, k * PIECE:(k + 1) * PIECE, D:D + P]
                            pool.tensor_tensor(out=cols, in0=cols, in1=adj_ring[:, k % RING, :, :],
                                               op=ALU.add).then_inc(cols_added, 1)
                            pool.wait_ge(cols_added, t * NPIECE + (k + 1))
                else:
                    def rows(t):
                        pool.tensor_copy(stage[:, 0:2 * D].rearrange("p (a d) -> p a d", a=1), big[:, at(t), :]).then_inc(copied, 1)
                        pool.tensor_copy(stage[:, 2 * D:3 * D].rearrange("p (a d) -> p a d", a=1), nodes[:, at(t), 0:D]).then_inc(copied, 1)

                    def load_hx(t):
                        pool.dma_start(h_in.rearrange("p (a d) -> p a d", a=1), h_dram[:, at(t), :]).then_inc(hx_loaded, 16)
                        pool.dma_start(x_in, x[bass.ds(t * P, P), :]).then_inc(hx_loaded, 16)

                    pool.wait_ge(big_ready, T)
                    rows(0)
                    load_hx(0)
                    with pool.Fori(1, T) as t:
                        pool.wait_ge(xt_used, batches(t, s))
                        rows(t)
                        pool.wait_ge(o_ready, t)
                        pool.dma_start(out[bass.ds(t * P - P, P), :], x_in).then_inc(o_stored, 16)
                        pool.wait_ge(o_stored, t * 16)
                        load_hx(t)
            pool.wait_ge(o_ready, T)
            pool.dma_start(out[(T - 1) * P:T * P, :], x_in).then_inc(o_stored, 16)
            pool.wait_ge(o_stored, 16 * T)

        @block.scalar
        def _(act):
            act.wait_ge(var_ready, 1)
            nc.scalar.activation(ln_b[:, :], ln_a[:, :], ACT.Sqrt).then_inc(std_ready, 1)
            act.wait_ge(affine_ready, 1)
            with act.Fori(0, T) as t:
                row = nodes[:, at(t), 0:D]
                act.activation(row, row, ACT.Relu, bias=ln_b[:, at(t)], scale=ln_a[:, at(t)]).then_inc(h_ready, 1)
            for s in range(2):
                with act.Fori(0, NGROUP) as g:
                    for c in range(DC):
                        act.wait_ge(p_tr_full, g * 2 + (2 * NGROUP * s + c + 1))
                        act.activation(xt[:, c, :], tr[:, c, :], ACT.Copy).then_inc(p_xt_ready, 1)
                    act.wait_ge(kt_full, g + (NGROUP * s + 1))
                    act.activation(t1, logits[0:DA, 0, BANK:2 * BANK], ACT.Copy).then_inc(t1_ready, 1)
                    act.activation(k_stack[:, bass.ds(g * BANK, BANK)], logits[:, 0, 0:BANK], ACT.Copy).then_inc(kq_hi, 1)
                    act.wait_ge(q_full, g + (NGROUP * s + 1))
                    act.activation(q_parts[:, 0:BANK].bitcast(F32R), logits[:, 1, 0:BANK], ACT.Copy).then_inc(kq_hi, 1)
                    act.wait_ge(q_stored, g * 16 + (NGROUP * s + 1) * 16)

                def exps(t, b):
                    act.wait_ge(negmax_ready, t + (T * s + 1))
                    act.activation(probs[:, b, :], probs[:, b, :], ACT.Exp, bias=negmax[:, b:b + 1],
                                   accum_out=zsum[:, b:b + 1]).then_inc(exp_done, 1)

                def to_sbuf(t, k):
                    act.wait_ge(tr_full, batches(t, s) + (k + 1))
                    act.wait_ge(xt_used, batches(t, s) + batch_free(k))
                    act.activation(xt[:, k % 2, :], tr[:, k % 2, :], ACT.Copy).then_inc(xt_ready, 1)

                def inverse_std(t):
                    act.wait_ge(var2_ready, t + 1)
                    act.activation(fin[:, 1:2], fin[:, 0:1], ACT.Ln).then_inc(log_done, 1)
                    act.wait_ge(log_done, t + 1)
                    act.activation(fin[:, 2:3], fin[:, 1:2], ACT.Exp, scale=-0.5).then_inc(rstd_ready, 1)

                def tile(t, b, last=False):
                    if not last:
                        exps(t + 1, 1 - b)
                    if s and not (isinstance(t, int) and t == 0):
                        inverse_std(t - 1)
                    for k in range(NTB):
                        to_sbuf(t, k)
                    act.wait_ge(xt_used, batches(t, s) + NTB)
                    if s == 0:
                        act.wait_ge(xa_stored, t * 16)
                        act.activation(xa_out[:, b, :], acc[:, 0, :], ACT.Copy,
                                       scale=rkept[:, b:b + 1]).then_inc(xa_ready, 1)
                        act.wait_ge(xa_ready, t + 1)
                        act.dma_start(xa_dram[at(t), :, :], xa_out[:, b, :]).then_inc(xa_stored, 16)
                    else:
                        act.activation(stage[:, 5 * D:6 * D], acc[:, 0, :], ACT.Copy,
                                       scale=rkept[:, b:b + 1]).then_inc(xa_ready, 1)
                        for k in range(NTB, NTB + UB):
                            to_sbuf(t, k)

                exps(0, 0)
                tile(0, 0)
                with act.Fori(0, T // 2 - 1) as i:
                    tile(i * 2 + 1, 1)
                    tile(i * 2 + 2, 0)
                tile(T - 1, 1, last=True)
                if s == 0:
                    act.wait_ge(cinv_ready, 1)
                    with act.Fori(0, T) as t:
                        act.activation(big[:, at(t), D:2 * D], big[:, at(t), 0:D], ACT.Copy,
                                       scale=cinv[:, at(t)]).then_inc(xb_ready, 1)
                else:
                    inverse_std(T - 1)

        @block.tensor
        def _(pe):
            pe.wait_ge(w_loaded, 16 * 13)
            pe.wait_ge(consts, 4)
            for s in range(2):
                with pe.Fori(0, NGROUP) as g:
                    pe.wait_ge(staged, g + (NGROUP * s + 1))
                    for c in range(DC):
                        for j in range(GROUP):
                            ins = nc.tensor.transpose(tr[:, c, j * P:(j + 1) * P],
                                                      stage[:, j * D + c * P:j * D + (c + 1) * P], ident[:, :])
                        ins.then_inc(p_tr_full, 1)
                    pe.wait_ge(p_xt_ready, g * 2 + (NGROUP * s * 2 + 2))
                    for c in range(DC):
                        nc.tensor.matmul(logits[:, 0, 0:BANK], w3d[:, c, :], xt[:, c, :], start=c == 0, stop=c == DC - 1)
                    for c in range(DC):
                        ins = nc.tensor.matmul(logits[0:DA, 0, BANK:2 * BANK], w1[:, c, :], xt[:, c, :],
                                               start=c == 0, stop=c == DC - 1)
                    ins.then_inc(kt_full, 1)
                    pe.wait_ge(t1_ready, g + (NGROUP * s + 1))
                    nc.tensor.matmul(logits[:, 1, 0:BANK], w2d[:, :], t1, start=True, stop=True).then_inc(q_full, 1)
                    pe.wait_ge(kq_done, g * 2 + (NGROUP * s * 2 + 2))
                if s == 1:
                    pe.wait_ge(big_ready, T)

                def logit_rows(t, b, loads):
                    pe.wait_ge(q_loaded[b], loads * 16 + T // 2 * s * 16)
                    for k in range(LCH):
                        n = t * LCH + (T * s * LCH + k)
                        if not isinstance(t, int) or n >= 2:
                            pe.wait_ge(logits_free, n - 1)
                        for j in range(LW // BANK):
                            cols = slice(k * LW + j * BANK, k * LW + (j + 1) * BANK)
                            o = logits[:, k % 2, j * BANK:(j + 1) * BANK]
                            nc.tensor.matmul(o, q_tile[:, b, 0, :], k_stack[:, cols], start=True, stop=False)
                            ins = nc.tensor.matmul(o, q_tile[:, b, 1, :], k_stack[:, cols], start=False, stop=True)
                        ins.then_inc(logits_full, 1)

                def adj_rows(t):
                    pe.wait_ge(sx_read, t + T * s)
                    width = D + 1 if s == 0 else 2 * D
                    src = nodes if s == 0 else big
                    for k in range(NPIECE):
                        pe.wait_ge(adj_loaded[k % RING],
                                   t * (16 * NPIECE // RING) + (T * s * NPIECE // RING + k // RING + 1) * 16)
                        for c in range(PIECE):
                            ch = k * PIECE + c
                            ins = nc.tensor.matmul(sx[:, 0:width], adj_ring[:, k % RING, c, :], src[:, ch, 0:width],
                                                   start=ch == 0, stop=ch == T - 1)
                        ins.then_inc(adj_used, 1)

                def batch(t, k, block_of):
                    pe.wait_ge(xt_ready, batches(t, s) + batch_free(k))
                    for j in range(TB):
                        ins = nc.tensor.transpose(tr[:, k % 2, j * P:(j + 1) * P], block_of(k, j), ident[:, :])
                    ins.then_inc(tr_full, 1)

                def attend(t, b):
                    def block_of(k, j):
                        return probs[:, b, (k * TB + j) * P:(k * TB + j + 1) * P]

                    pe.wait_ge(masked, t + (T * s + 1))
                    batch(t, 0, block_of)
                    pe.wait_ge(xa_ready, t + T * s)
                    for k in range(NTB):
                        if k + 1 < NTB:
                            batch(t, k + 1, block_of)
                        pe.wait_ge(xt_ready, batches(t, s) + (k + 1))
                        for j in range(TB):
                            ch = k * TB + j
                            ins = nc.tensor.matmul(acc[:, 0, :], xt[:, k % 2, j * P:(j + 1) * P], nodes[:, ch, 0:D],
                                                   start=ch == 0, stop=ch == T - 1)
                        ins.then_inc(xt_used, 1)

                def u_products(t):
                    def block_of(k, j):
                        n = (k - NTB) * TB + j
                        return stage[:, n * P:(n + 1) * P]

                    pe.wait_ge(copied, t * 2 + 2)
                    pe.wait_ge(sx_read, t + (T + 1))
                    pe.wait_ge(xa_ready, t + (T + 1))
                    pe.wait_ge(y_read, t)
                    batch(t, NTB, block_of)
                    for k in range(NTB, NTB + UB):
                        if k + 1 < NTB + UB:
                            batch(t, k + 1, block_of)
                        pe.wait_ge(xt_ready, batches(t, s) + (k + 1))
                        for j in range(TB):
                            n = (k - NTB) * TB + j
                            ins = nc.tensor.matmul(acc[:, 1, :], xt[:, k % 2, j * P:(j + 1) * P],
                                                   u_all[:, n // DC, n % DC, :], start=n == 0, stop=n == UB * TB - 1)
                        ins.then_inc(xt_used, 1)

                def tile(t, b, last=False, loads=None):
                    if not last:
                        logit_rows(t + 1, 1 - b, loads)
                    adj_rows(t)
                    attend(t, b)
                    if s:
                        u_products(t)

                logit_rows(0, 0, 1)
                tile(0, 0, loads=1)
                with pe.Fori(0, T // 2 - 1) as i:
                    tile(i * 2 + 1, 1, loads=i + 2)
                    tile(i * 2 + 2, 0, loads=i + 2)
                tile(T - 1, 1, last=True)

        @block.vector
        def _(dve):
            v = nc.vector
            seq = Chain(dve, dve_seq)

            def carry_wait():
                v.tensor_copy(pad[:, 1:2], pad[:, 0:1])

            def variance(mean, var, half, stat):
                seq(v.tensor_tensor(mean, stat(1), stat(4), ALU.add))
                seq(v.tensor_scalar(mean, mean, 0.5, None, ALU.mult))
                seq(v.tensor_tensor(half, mean, stat(1), ALU.subtract))
                seq(v.tensor_tensor(half, half, half, ALU.mult))
                seq(v.tensor_tensor(var, stat(2), stat(5), ALU.add))
                seq(v.tensor_scalar(var, var, 1.0 / D, None, ALU.mult))
                seq(v.tensor_tensor(var, var, half, ALU.add))

            v.memset(flag[:, :], 0.0)
            seq(v.memset(pad[:, :], 0.0))
            dve.wait_ge(x_loaded, 16)
            with dve.Fori(0, T) as t:
                v.bn_stats(x_stats[:, at(t), :].rearrange("p a d -> p (a d)"),
                           nodes[:, at(t), 0:D].rearrange("p a d -> p (a d)")).then_inc(dve_seq, 1)
            seq.base, seq.k = T + 1, 0
            dve.wait_ge(dve_seq, T + 1)
            variance(x_mean, ln_a[:, :], ln_b[:, :], lambda k: x_stats[:, :, k])
            v.tensor_scalar(ln_a[:, :], ln_a[:, :], EPS, None, ALU.add).then_inc(var_ready, 1)
            dve.wait_ge(std_ready, 1)
            seq(v.reciprocal(ln_c[:, :], ln_b[:, :]))
            seq(v.tensor_tensor(ln_b[:, :], ln_c[:, :], ln_c[:, :], ALU.mult))
            seq(v.tensor_tensor(ln_b[:, :], ln_b[:, :], ln_a[:, :], ALU.mult))
            seq(v.tensor_scalar(ln_b[:, :], ln_b[:, :], -0.5, 1.5, ALU.mult, ALU.add))
            seq(v.tensor_tensor(ln_a[:, :], ln_c[:, :], ln_b[:, :], ALU.mult))
            seq(v.tensor_tensor(ln_b[:, :], x_mean, ln_a[:, :], ALU.mult))
            v.tensor_scalar(ln_b[:, :], ln_b[:, :], -1.0, None, ALU.mult).then_inc(affine_ready, 1)

            for s in range(2):
                with dve.Fori(0, NGROUP) as g:
                    kcols = bass.ds(g * BANK, BANK)
                    dve.wait_ge(kq_hi, g * 2 + (NGROUP * s * 2 + 1))
                    v.tensor_tensor(k_stack[DA:P, kcols], logits[DA:P, 0, 0:BANK], k_stack[DA:P, kcols].bitcast(F32),
                                    ALU.subtract).then_inc(kq_done, 1)
                    dve.wait_ge(kq_hi, g * 2 + (NGROUP * s * 2 + 2))
                    v.tensor_tensor(q_parts[:, BANK:2 * BANK].bitcast(F32R), logits[:, 1, 0:BANK], q_parts[:, 0:BANK],
                                    ALU.subtract).then_inc(kq_done, 1)

                def evacuate(t, b):
                    for k in range(LCH):
                        dve.wait_ge(logits_full, t * LCH + (T * s * LCH + k + 1))
                        v.tensor_scalar(probs[:, b, k * LW:(k + 1) * LW], logits[:, k % 2, :], 1.0, None, ALU.mult,
                                        ALU.max, accum_out=pmax[:, k:k + 1]).then_inc(logits_free, 1)
                    dve.wait_ge(logits_free, t * LCH + (T * s + 1) * LCH)
                    seq(v.reduce_max(negmax[:, b:b + 1], pmax[:, :], AX_X))
                    v.tensor_scalar(negmax[:, b:b + 1], negmax[:, b:b + 1], -1.0, None, ALU.mult)\
                        .then_inc(negmax_ready, 1)

                def finish(t):
                    dve.wait_ge(xt_used, batches(t + 1, 1))
                    dve.wait_ge(hx_loaded, (t + 1) * 32)
                    v.tensor_tensor(y_t[:, :], acc[:, 1, :], h_in, ALU.add).then_inc(y_read, 1)
                    dve.wait_ge(y_read, t + 1)
                    seq(v.bn_stats(bn[:, :], y_t[:, :]))
                    variance(fin[:, 4:5], fin[:, 5:6], fin[:, 3:4], lambda k: bn[:, k:k + 1])
                    v.tensor_scalar(fin[:, 0:1], fin[:, 5:6], EPS, None, ALU.add).then_inc(var2_ready, 1)
                    dve.wait_ge(rstd_ready, t + 1)
                    seq(v.tensor_scalar(fin[:, 3:4], fin[:, 2:3], fin[:, 2:3], fin[:, 0:1], ALU.mult, ALU.mult))
                    seq(v.tensor_scalar(fin[:, 3:4], fin[:, 3:4], -0.5, 1.5, ALU.mult, ALU.add))
                    seq(v.tensor_scalar(fin[:, 3:4], fin[:, 3:4], fin[:, 2:3], None, ALU.mult))
                    seq(v.tensor_scalar(y_t[:, :], y_t[:, :], fin[:, 4:5], fin[:, 3:4], ALU.subtract, ALU.mult))
                    seq(v.tensor_tensor(y_t[:, :], y_t[:, :], gam[:, :], ALU.mult))
                    seq(v.tensor_tensor(y_t[:, :], y_t[:, :], bet[:, :], ALU.add))
                    v.tensor_tensor(x_in, y_t[:, :], x_in, ALU.add).then_inc(o_ready, 1)

                def start_search(b):
                    seq(v.tensor_scalar(target, zsum[:, b:b + 1], P_NUC, None, ALU.mult))
                    v.tensor_scalar(lo[:, 0:1], zsum[:, b:b + 1], 0.99 * (1 - P_NUC) / N, None, ALU.mult)
                    v.tensor_scalar(lo[:, 1:2], zsum[:, b:b + 1], 1 - P_NUC, None, ALU.mult)
                    v.tensor_scalar(lo[:, 2:3], zsum[:, b:b + 1], 1.0, None, ALU.mult)
                    v.memset(hi[:, 0:1], 1.0001)
                    v.tensor_scalar(hi[:, 1:2], target, -1.0, None, ALU.mult)
                    v.memset(hi[:, 2:3], 0.0)
                    seq(v.tensor_scalar(new[:, 0:1], zsum[:, b:b + 1], (1 - P_NUC) / N, FIRST, ALU.mult, ALU.max))

                def weigh(b, q, edge=EDGE):
                    q(v.scalar_tensor_tensor(out=scratch[:, :], in0=probs[:, b, :], scalar=new[:, 0:1],
                                             in1=probs[:, b, :], op0=ALU.is_ge, op1=ALU.mult, accum_out=new[:, 2:3]))
                    mass = new[:, 2:3].to_broadcast([P, 3])
                    v.tensor_scalar(reaches[:, :], mass, target, None, ALU.is_ge)
                    v.tensor_scalar(misses[:, :], mass, target, None, ALU.is_lt)
                    v.tensor_scalar(lo[:, 1:2], lo[:, 1:2], FADE, None, ALU.mult)
                    v.tensor_scalar(hi[:, 1:2], hi[:, 1:2], FADE, None, ALU.mult)
                    q(v.tensor_tensor(new[:, 1:2], new[:, 2:3], target, ALU.subtract))
                    carry_wait()
                    v.copy_predicated(lo[:, :], reaches[:, :], new[:, :])
                    q(v.copy_predicated(hi[:, :], misses[:, :], new[:, :]))
                    v.scalar_tensor_tensor(out=numer, in0=lo[:, 0:1], scalar=-AIM, in1=lo[:, 1:2], op0=ALU.mult, op1=ALU.subtract)
                    q(v.tensor_tensor(gap, hi[:, 0:2], lo[:, 0:2], ALU.subtract))
                    q(v.reciprocal(ratio, gap[:, 1:2]))
                    q(v.tensor_scalar(ratio, ratio, numer, edge, ALU.mult, ALU.max))
                    q(v.scalar_tensor_tensor(out=ratio, in0=ratio, scalar=1 - edge, in1=gap[:, 0:1], op0=ALU.min, op1=ALU.mult))
                    q(v.tensor_tensor(new[:, 0:1], ratio, lo[:, 0:1], ALU.add))

                def passes(b, count):
                    base, k = seq.base, seq.k
                    carry_wait()
                    with dve.Fori(0, count) as j:
                        seq.base, seq.k = j * SEQ_PER_PASS + (base + k), 0
                        weigh(b, seq)
                        assert seq.k == SEQ_PER_PASS, seq.k
                    seq.base, seq.k = base, k + SEQ_PER_PASS * count

                def settle(b, q):
                    q(v.scalar_tensor_tensor(out=scratch[:, :], in0=probs[:, b, :], scalar=hi[:, 0:1],
                                             in1=probs[:, b, :], op0=ALU.is_lt, op1=ALU.mult))
                    carry_wait()
                    q(v.max(best[:, 0:8], scratch[:, :]))
                    v.tensor_copy(best[:, 8:9], best[:, 7:8])
                    q(v.tensor_tensor_scan(best_sum[:, :], best[:, 0:8], best[:, 0:8], hi[:, 2:3], ALU.add, ALU.max))
                    v.tensor_copy(best_ok[:, 8:9], best[:, 8:9])
                    q(v.scalar_tensor_tensor(out=best_ok[:, 0:8], in0=best_sum[:, :], scalar=target, in1=best[:, 0:8],
                                             op0=ALU.is_ge, op1=ALU.mult))
                    q(v.reduce_max(thr, best_ok[:, :], AX_X))
                    v.tensor_scalar(best_ok[:, :], best[:, :], thr, None, ALU.is_equal, ALU.add, accum_out=flag[:, 0:1])
                    v.tensor_scalar(negthr, thr, -1.0, None, ALU.mult)
                    q(v.scalar_tensor_tensor(out=best_sum[:, :], in0=best[:, 0:8], scalar=thr, in1=best[:, 0:8],
                                             op0=ALU.is_gt, op1=ALU.mult, accum_out=above))
                    q(v.tensor_tensor(above, above, hi[:, 2:3], ALU.add))

                def any_flag(q):
                    q(v.transpose(flag_t[:, :], flag[:, :]))
                    q(v.reduce_max(flag_q[:, 0:1], flag_t[:, :], AX_X))
                    v.tensor_copy(flag_q[0:32, 1:2], flag_q[32:64, 0:1])
                    v.tensor_copy(flag_q[0:32, 2:3], flag_q[64:96, 0:1])
                    q(v.tensor_copy(flag_q[0:32, 3:4], flag_q[96:128, 0:1]))
                    q(v.reduce_max(flag_i[0:32, :], flag_q[0:32, :], AX_X))
                    carry_wait()
                    return dve.value_load(flag_i[0:1, 0:1], min_val=0, max_val=9)

                def ties(b, q):
                    v.reciprocal(ratio, thr)
                    q(v.tensor_scalar(tied, probs[:, b, :], thr, None, ALU.is_equal))
                    q(v.tensor_scalar(numer, target, above, ratio, ALU.subtract, ALU.mult))
                    q(v.tensor_tensor_scan(rank, tied, tied, 0.0, ALU.add, ALU.max))
                    v.tensor_scalar(limit, numer, 1.0, 1.5, ALU.add, ALU.max)
                    q(v.scalar_tensor_tensor(out=flag[:, 0:1], in0=numer, scalar=-ROOM, in1=rank[:, N - 1:N],
                                             op0=ALU.add, op1=ALU.is_gt))

                def drop_ties(b, q):
                    q(v.scalar_tensor_tensor(out=tied, in0=rank, scalar=limit, in1=tied, op0=ALU.is_ge, op1=ALU.mult))
                    q(v.scalar_tensor_tensor(out=probs[:, b, :], in0=tied, scalar=negthr, in1=probs[:, b, :],
                                             op0=ALU.mult, op1=ALU.add))

                def resolve(b, q):
                    ties(b, q)
                    with dve.If(any_flag(q) > 0):
                        with dve.Fori(0, ROUNDS):
                            with dve.If(dve.value_load(flag_i[0:1, 0:1], min_val=0, max_val=9) > 0):
                                rnd = Chain(dve, round_seq)
                                for n in range(ROUND_PASSES):
                                    weigh(b, rnd, edge=0.5 if n == ROUND_PASSES - 2 else EDGE)
                                settle(b, rnd)
                                ties(b, rnd)
                                any_flag(rnd)
                                dve.sem_clear(round_seq)
                    drop_ties(b, q)

                def read_adj_product(t, first):
                    dve.wait_ge(adj_used, (t + 1) * NPIECE + T * s * NPIECE)
                    if s == 0:
                        seq(v.tensor_tensor(big[:, at(t), 0:D].rearrange("p a d -> p (a d)"), sx[:, 0:D],
                                            nodes[:, at(t), 0:D].rearrange("p a d -> p (a d)"), ALU.add))
                        v.tensor_scalar(rinv[:, at(t)], sx[:, D:D + 1], 1.0, 1e-12, ALU.add, ALU.max)\
                            .then_inc(sx_read, 1)
                        return
                    if not first:
                        dve.wait_ge(xt_used, batches(t, s))
                    seq(v.tensor_tensor(stage[:, 3 * D:5 * D], sx[:, :],
                                        big[:, at(t), :].rearrange("p a d -> p (a d)"), ALU.add))
                    seq(v.tensor_scalar(stage[:, 3 * D:4 * D], stage[:, 3 * D:4 * D], rinv[:, at(t)], None, ALU.mult))
                    v.tensor_scalar(stage[:, 4 * D:5 * D], stage[:, 4 * D:5 * D], cinv[:, at(t)], None, ALU.mult)\
                        .then_inc(sx_read, 1)

                def mask(t, b):
                    settle(b, seq)
                    if s == 0:
                        with dve.If(any_flag(seq) > 1):
                            tie = Chain(dve, tie_seq)
                            resolve(b, tie)
                            dve.sem_clear(tie_seq)
                    else:
                        resolve(b, seq)
                    seq(v.scalar_tensor_tensor(out=probs[:, b, :], in0=probs[:, b, :], scalar=thr, in1=probs[:, b, :],
                                               op0=ALU.is_ge, op1=ALU.mult, accum_out=kept))
                    v.reciprocal(rkept[:, b:b + 1], kept).then_inc(masked, 1)

                def tile(t, b, first=False, last=False):
                    dve.wait_ge(exp_done, t + (T * s + 1))
                    start_search(b)
                    passes(b, PASSES[s] // 2)
                    if not last:
                        if not first:
                            dve.wait_ge(tr_full, batches(t, s) - (UB if s else 0))
                        evacuate(t + 1, 1 - b)
                    passes(b, PASSES[s] - PASSES[s] // 2)
                    read_adj_product(t, first)
                    if s and not first:
                        finish(t - 1)
                    mask(t, b)

                evacuate(0, 0)
                tile(0, 0, first=True)
                seq.base, seq.k = seq.base + seq.k, 0
                base = seq.base
                per = SEQ_PER_TILE[s]
                with dve.Fori(0, T // 2 - 1) as i:
                    seq.base, seq.k = i * (2 * per) + base, 0
                    tile(i * 2 + 1, 1)
                    assert seq.k == per, seq.k
                    tile(i * 2 + 2, 0)
                seq.base, seq.k = base + (T - 2) * per, 0
                tile(T - 1, 1, last=True)
                if s == 0:
                    dve.wait_ge(cols_added, T * NPIECE)
                    seq(v.reduce_sum(cinv[:, :], big[:, :, D:D + P], AX_X))
                    seq(v.tensor_scalar(cinv[:, :], cinv[:, :], 1.0, 1e-12, ALU.add, ALU.max))
                    seq(v.reciprocal(rinv[:, :], rinv[:, :]))
                    v.reciprocal(cinv[:, :], cinv[:, :]).then_inc(cinv_ready, 1)
                    with dve.Fori(0, T) as t:
                        dve.wait_ge(xb_ready, t + 1)
                        v.tensor_scalar(big[:, at(t), 0:D], big[:, at(t), 0:D], rinv[:, at(t)], None, ALU.mult)\
                            .then_inc(big_ready, 1)
                else:
                    finish(T - 1)


def kernel(x, adj, L0_gnn_W1, L0_gnn_W2, L0_gnn_W3, L0_gnn_U1, L0_gnn_U2, L0_gnn_U3, L0_gnn_gamma, L0_gnn_beta):
    import concourse.bacc as bacc
    from concourse.bass_utils import run_bass_kernel_spmd

    def arr(a):
        return np.ascontiguousarray(np.asarray(a))

    arrays = {
        "x_in_dram": arr(x),
        "adj_t_dram": arr(np.asarray(adj).reshape(T, P, T, P).transpose(0, 3, 2, 1)),
        "w1_dram": arr(L0_gnn_W1), "w2_dram": arr(L0_gnn_W2), "w3_dram": arr(L0_gnn_W3),
        "u1_dram": arr(L0_gnn_U1), "u2_dram": arr(L0_gnn_U2), "u3_dram": arr(L0_gnn_U3),
        "gamma_dram": arr(np.broadcast_to(np.asarray(L0_gnn_gamma), (P, D))),
        "beta_dram": arr(np.broadcast_to(np.asarray(L0_gnn_beta), (P, D))),
    }
    nc = bacc.Bacc("TRN2", target_bir_lowering=False, num_devices=1)
    args = [nc.dram_tensor(n, a.shape, mybir.dt.from_np(a.dtype), kind="ExternalInput").ap()
            for n, a in arrays.items()]
    out = nc.dram_tensor("out_dram", (N, D), F32, kind="ExternalOutput").ap()
    build(nc, *args, out)
    r = run_bass_kernel_spmd(nc, [arrays], core_ids=[0])
    return r.results[0]["out_dram"]
```

```python
import numpy as np
import concourse.bass as bass
from concourse import mybir
from contextlib import ExitStack

F32 = mybir.dt.float32
F32R = mybir.dt.float32r
BF16 = mybir.dt.bfloat16
U16 = mybir.dt.uint16
U32 = mybir.dt.uint32
ALU = mybir.AluOpType
ACT = mybir.ActivationFunctionType
AX_X = mybir.AxisListType.X

P = 128
N = 4096
D = 256
DC = D // P
DA = 64
T = N // P
LW = 1024
LCH = N // LW
BANK = 512
TB = 4
NTB = T // TB
UB = 6 * DC // TB
ROOM = 0.05
SEQ_PER_TILE = (38, 74)
PIECE = 4
NPIECE = T // PIECE
RING = 4
GROUP = 4
NGROUP = T // GROUP
P_NUC = 0.9
EPS = 1e-5
PARTS = 4
BUFS = 3
BODY = (T - 5) // BUFS
FIRST = (0.025, 0.01)
LADDER = ((4.0, 2.0, 1.4), (4.0, 2.0, 1.4, 1.2))
NLAD = tuple(len(factors) + 1 for factors in LADDER)
AIM = 3.0
FADE = 0.7
EDGE = 0.02
PASSES = (2, 5)
BETWEEN = ((2, 4, 5, 7), (3, 5, 7))
ROUND_PASSES = 4
ROUNDS = 44
TOP = 1.0001
FAR = 1e5
SLACK = 4e-6


class Chain:

    def __init__(self, eng, sem):
        self.eng, self.sem, self.base, self.k = eng, sem, 0, 0

    def __call__(self, ins):
        self.mark(ins)
        self.wait()

    def mark(self, ins):
        ins.then_inc(self.sem, 1)
        self.k += 1

    def wait(self):
        self.eng.wait_ge(self.sem, self.base + self.k)


def build(nc, x, adj_t, W1, W2, W3, U1, U2, U3, gamma, beta, out):
    ctx = ExitStack()
    with ctx:
        def sb(name, shape, dt=F32):
            return ctx.enter_context(nc.sbuf_tensor(name, shape, dt))

        def ps(name, shape):
            return ctx.enter_context(nc.psum_tensor(name, shape, F32))

        def sem(name):
            return ctx.enter_context(nc.semaphore(name))

        h_dram = nc.dram_tensor("h_dram", [P, T, D], F32).ap()
        xa_dram = nc.dram_tensor("xa_dram", [T, P, D], F32).ap()
        q_dram = nc.dram_tensor("q_dram", [2, T, P, 2, P], F32).ap()

        nodes = sb("nodes", [P, T, D + 1])
        big = sb("big", [P, T, 2 * D])
        k_stack = sb("k_stack", [P, N], F32R)
        q_tile = sb("q_tile", [P, BUFS, 2, P], F32R)
        probs = sb("probs", [P, BUFS, N])
        dump = sb("dump", [P, N], mybir.dt.int8)
        adj_ring = sb("adj_ring", [P, RING, PIECE, P])
        scratch = sb("scratch", [P, N])
        tied = scratch[:, 0:N // 2].bitcast(BF16)
        rank = scratch[:, N // 2:N].bitcast(U16)
        xt = sb("xt", [P, 2, BANK])
        stage = sb("stage", [P, 6 * D])
        w3d = sb("w3d", [P, DC, P])
        w1 = sb("w1", [P, DC, DA])
        w2d = sb("w2d", [DA, P])
        t1 = stage[0:DA, 4 * D:6 * D]
        q_parts = probs[:, 0:2, :]
        groups = [scratch[:, k * GROUP * D:(k + 1) * GROUP * D] for k in range(2)]
        u_all = sb("u_all", [P, 6, DC, D])
        ident = sb("ident", [P, P])
        gam = sb("gam", [P, D])
        bet = sb("bet", [P, D])
        xa_out = sb("xa_out", [P, 2, D])
        h_in = y_t = xa_out[:, 0, :]
        x_in = xa_out[:, 1, :]
        bn = sb("bn", [P, 6])
        ln_a = sb("ln_a", [P, T])
        rinv = sb("rinv", [P, T])
        cinv = sb("cinv", [P, T])
        ln_b, ln_c = rinv, cinv
        x_stats = stage[:, 0:6 * T].rearrange("p (t k) -> p t k", k=6)
        x_mean = stage[:, 6 * T:7 * T]
        small = sb("small", [P, 35])
        part_min = sb("part_min", [P, BUFS, LCH])
        negmax = small[:, 4:7]
        zsum = small[:, 7:10]
        rkept = small[:, 10:13]
        target = small[:, 13:14]
        thr = small[:, 14:15]
        negthr = small[:, 15:16]
        above = small[:, 16:17]
        limit = small[:, 17:18]
        kept = small[:, 18:19]
        numer = small[:, 19:20]
        ratio = small[:, 20:21]
        gap = small[:, 21:23]
        below = small[:, 23:24]
        upper = small[:, 24:25]
        way, least, most, slack = (small[:, k:k + 1] for k in (25, 32, 33, 34))
        fin = small[:, 26:32]
        lo = sb("lo", [P, 2])
        hi = sb("hi", [P, 2])
        new = sb("new", [P, 3])
        reaches = sb("reaches", [P, 2], U32)
        misses = sb("misses", [P, 2], U32)
        lad = sb("lad", [P, BUFS, 4, max(NLAD)])
        lad_p = sb("lad_p", [P, 5])
        ends = sb("ends", [P, 4, max(NLAD) + 1])
        lad_v = sb("lad_v", [P, 3, max(NLAD)])
        best = sb("best", [P, 9])
        best_sum = sb("best_sum", [P, 8])
        best_ok = sb("best_ok", [P, 9])
        flag = sb("flag", [P, 32])
        flag_t = sb("flag_t", [P, 32])
        pad = sb("pad", [P, 2])
        flag_q = sb("flag_q", [P, 4])
        flag_i = sb("flag_i", [P, 1], mybir.dt.int32)

        logits = ps("logits", [P, 2, LW])
        tr = ps("tr", [P, 2, BANK])
        acc = ps("acc", [P, 2, D])
        sx = ps("sx", [P, BANK])

        x_loaded = [sem(f"x_loaded{k}") for k in range(PARTS)]
        w_loaded = sem("w_loaded")
        consts = sem("consts")
        var_ready = sem("var_ready")
        std_ready = sem("std_ready")
        affine_ready = sem("affine_ready")
        h_ready = sem("h_ready")
        h_stored = sem("h_stored")
        staged = sem("staged")
        p_tr_full = sem("p_tr_full")
        p_xt_ready = sem("p_xt_ready")
        t1_full = sem("t1_full")
        k_full = sem("k_full")
        t1_ready = sem("t1_ready")
        q_full = sem("q_full")
        kq_hi = sem("kq_hi")
        kq_done = sem("kq_done")
        q_stored = sem("q_stored")
        q_loaded = [sem(f"q_loaded{b}") for b in range(BUFS)]
        logits_full = sem("logits_full")
        logits_free = sem("logits_free")
        negmax_ready = sem("negmax_ready")
        exp_done = sem("exp_done")
        point_set = sem("point_set")
        relu_summed = sem("relu_summed")
        point_weighed = sem("point_weighed")
        masked = sem("masked")
        tr_full = sem("tr_full")
        xt_ready = sem("xt_ready")
        xt_used = sem("xt_used")
        xa_ready = sem("xa_ready")
        xa_stored = sem("xa_stored")
        xa_back = sem("xa_back")
        adj_loaded = [sem(f"adj_loaded{s}") for s in range(RING)]
        adj_used = sem("adj_used")
        cols_added = sem("cols_added")
        sx_read = sem("sx_read")
        xb_ready = sem("xb_ready")
        cinv_ready = sem("cinv_ready")
        big_ready = sem("big_ready")
        copied = sem("copied")
        y_read = sem("y_read")
        hx_loaded = sem("hx_loaded")
        var2_ready = sem("var2_ready")
        log_done = sem("log_done")
        rstd_ready = sem("rstd_ready")
        o_ready = sem("o_ready")
        o_stored = sem("o_stored")
        pool_seq = sem("pool_seq")
        dve_seq = sem("dve_seq")
        tie_seq = sem("tie_seq")
        round_seq = sem("round_seq")

        block = ctx.enter_context(nc.Block())

        def loads(u, s):
            return len(range(u % BUFS, T, BUFS)) * s

        def weighed(t, s):
            return t * NLAD[s] + (T * NLAD[0] if s else 0)

        def batches(t, s):
            return t * (NTB + UB) + T * NTB if s else t * NTB

        def batch_free(k):
            return k - 1 if k >= 2 else 0

        def at(t):
            return bass.ds(t, 1)

        @block.sync
        def _(sp):
            for k in range(PARTS):
                ts = slice(k * T // PARTS, (k + 1) * T // PARTS)
                sp.dma_start(nodes[:, ts, 0:D], x.rearrange("(t p) d -> p t d", p=P)[:, ts, :]).then_inc(x_loaded[k], 16)
            sp.dma_start(w1[:, :, :], W1.rearrange("(c p) n -> p c n", p=P)).then_inc(w_loaded, 16)
            for half in range(2):
                cols = slice(half * DA, (half + 1) * DA)
                sp.dma_start(w3d[:, :, cols], W3.rearrange("(c p) n -> p c n", p=P)).then_inc(w_loaded, 16)
                sp.dma_start(w2d[:, cols], W2).then_inc(w_loaded, 16)
            for s in range(2):
                for j, U in enumerate((U1, U2, U3)):
                    sp.dma_start(u_all[:, 3 * s + j, :, :],
                                 U[s, :, :].rearrange("(c p) n -> p c n", p=P)).then_inc(w_loaded, 16)
            sp.dma_start(gam[:, :], gamma).then_inc(w_loaded, 16)
            sp.dma_start(bet[:, :], beta).then_inc(w_loaded, 16)
            sp.wait_ge(h_ready, T)
            sp.dma_start(h_dram, nodes[:, :, 0:D]).then_inc(h_stored, 16)
            for s in range(2):
                with sp.Fori(0, NGROUP) as g:
                    sp.wait_ge(kq_done, g * 2 + (2 * NGROUP * s + 2))
                    for h in range(2):
                        sp.dma_start(q_dram[s, bass.ds(g * GROUP, GROUP), :, h, :].rearrange("j p n -> p j n"),
                                     q_parts[:, h, bass.ds(g * BANK, BANK)].rearrange("p (j n) -> p j n", j=GROUP)).then_inc(q_stored, 16)
                sp.wait_ge(q_stored, 32 * NGROUP * (s + 1))

                def load_q(u, b):
                    sp.dma_start(q_tile[:, b, :, :].bitcast(F32), q_dram[s, at(u), :, :, :]).then_inc(q_loaded[b], 16)

                def load_adj(t, pieces):
                    for k in pieces:
                        n = t * NPIECE + (T * s * NPIECE + k)
                        if not isinstance(t, int) or n >= RING:
                            sp.wait_ge(adj_used, n + (1 - RING))
                            if s == 0:
                                sp.wait_ge(cols_added, n + (1 - RING))
                        sp.dma_start(adj_ring[:, k % RING, :, :],
                                     adj_t[at(t), :, k * PIECE:(k + 1) * PIECE, :]).then_inc(adj_loaded[k % RING], 16)

                def finish_rows(t):
                    if not isinstance(t, int) or t > 0:
                        sp.wait_ge(o_ready, t)
                        sp.dma_start(out[bass.ds(t * P - P, P), :], x_in).then_inc(o_stored, 16)
                        sp.wait_ge(o_stored, t * 16)
                    sp.dma_start(h_in.rearrange("p (a d) -> p a d", a=1), h_dram[:, at(t), :]).then_inc(hx_loaded, 16)
                    sp.dma_start(x_in, x[bass.ds(t * P, P), :]).then_inc(hx_loaded, 16)

                def tile(t, b, last=False):
                    if not last:
                        if not isinstance(t, int) or t > 0:
                            sp.wait_ge(logits_full, t * LCH + T * s * LCH)
                        load_q(t + 2, (b + 2) % BUFS)
                    load_adj(t, range(RING))
                    if s == 1 and not (isinstance(t, int) and t == 0):
                        finish_rows(t - 1)
                    load_adj(t, range(RING, NPIECE))

                if s == 1:
                    sp.wait_ge(logits_full, LCH * T)
                    sp.wait_ge(cols_added, T * NPIECE)
                load_q(0, 0)
                load_q(1, 1)
                tile(0, 0)
                tile(1, 1)
                with sp.Fori(0, BODY) as i:
                    for k in range(2, BUFS + 2):
                        tile(i * BUFS + k, k % BUFS)
                for t in range(T - 3, T):
                    tile(t, t % BUFS, last=t >= T - 2)
                if s == 0:
                    sp.wait_ge(xa_stored, 16 * T)
                    sp.wait_ge(sx_read, T)
                    sp.wait_ge(xt_used, T * NTB)
                    sp.wait_ge(h_stored, 16)
                    sp.dma_start(nodes[:, :, 0:D], xa_dram.rearrange("t p d -> p t d")).then_inc(xa_back, 16)
            finish_rows(T - 1)
            sp.wait_ge(o_ready, T)
            sp.dma_start(out[(T - 1) * P:T * P, :], x_in).then_inc(o_stored, 16)
            sp.wait_ge(o_stored, 16 * T)

        @block.gpsimd
        def _(pool):
            def carry_wait():
                pool.tensor_tensor(out=lad_p[:, 4:5], in0=ident[:, 0:1], in1=ident[:, 0:1], op=ALU.mult)

            pool.memset(ident[:, :], 0.0).then_inc(consts, 1)
            pool.memset(nodes[:, :, D:D + 1], 1.0).then_inc(consts, 1)
            pool.memset(big[:, :, D:D + P], 0.0).then_inc(consts, 1)
            pool.wait_ge(consts, 3)
            pool.affine_select(out=ident[:, :], in_=ident[:, :], compare_op=ALU.not_equal, fill=1.0, base=0,
                               pattern=[[-1, P]], channel_multiplier=1).then_inc(consts, 1)
            for s in range(2):
                if s == 1:
                    pool.wait_ge(xa_back, 16)

                def copy_group(g, b):
                    if s == 0:
                        pool.wait_ge(h_ready, g * GROUP + GROUP)
                    if not isinstance(g, int) or g >= 2:
                        pool.wait_ge(p_tr_full, g * 2 + (2 * NGROUP * s - 2))
                    pool.tensor_copy(groups[b].rearrange("p (j d) -> p j d", d=D),
                                     nodes[:, bass.ds(g * GROUP, GROUP), 0:D]).then_inc(staged, 1)

                copy_group(0, 0)
                copy_group(1, 1)
                with pool.Fori(1, NGROUP // 2) as i:
                    for k in range(2):
                        copy_group(i * 2 + k, k)

                def add_columns(t, pieces):
                    for k in pieces:
                        pool.wait_ge(adj_loaded[k % RING], t * (16 * NPIECE // RING) + 16 * (k // RING + 1))
                        cols = big[:, k * PIECE:(k + 1) * PIECE, D:D + P]
                        pool.tensor_tensor(out=cols, in0=cols, in1=adj_ring[:, k % RING, :, :],
                                           op=ALU.add).then_inc(cols_added, 1)
                        pool.wait_ge(cols_added, t * NPIECE + (k + 1))

                def ladder(u, b, columns_of=None):
                    goal, mass, count, move = (lad_p[:, k:k + 1] for k in range(4))
                    pool.wait_ge(exp_done, u + (T * s + 1))
                    carry_wait()
                    seq = Chain(pool, pool_seq)
                    seq.mark(pool.tensor_scalar(goal, zsum[:, b:b + 1], P_NUC, None, ALU.mult))
                    seq(pool.tensor_scalar(lad[:, b, 0, 0:1], zsum[:, b:b + 1], (1 - P_NUC) / N, FIRST[s],
                                           ALU.mult, ALU.max))
                    pool.tensor_scalar(lad[:, b, 1, 0:1], lad[:, b, 0, 0:1], -1.0, None, ALU.mult).then_inc(point_set, 1)
                    for e in range(NLAD[s]):
                        if e:
                            pool.wait_ge(point_weighed, weighed(u, s) + e)
                            carry_wait()
                            seq.wait()
                            point, minus, above, signs = (lad[:, b, k, e - 1:e] for k in range(4))
                            up, down = LADDER[s][e - 1], 1 / LADDER[s][e - 1]
                            seq(pool.tensor_scalar(count, signs, 0.5, N / 2, ALU.mult, ALU.add))
                            seq(pool.tensor_scalar(mass, count, point, above, ALU.mult, ALU.add))
                            seq(pool.tensor_scalar(move, mass, goal, up - down, ALU.is_ge, ALU.mult))
                            seq.mark(pool.tensor_scalar(lad[:, b, 0, e:e + 1], move, down, point, ALU.add, ALU.mult))
                            pool.tensor_scalar(lad[:, b, 1, e:e + 1], move, down, minus, ALU.add, ALU.mult)\
                                .then_inc(point_set, 1)
                        if e == 0 and columns_of is not None:
                            add_columns(columns_of, range(RING))
                    seq.wait()
                    pool.sem_clear(pool_seq)

                if s == 0:
                    def tile(t, b, last=False):
                        add_columns(t, range(RING, NPIECE))
                        if not last:
                            ladder(t + 2, (b + 2) % BUFS, columns_of=t + 1)
                        elif t < T - 1:
                            add_columns(t + 1, range(RING))
                else:
                    pool.wait_ge(big_ready, T)

                    def tile(t, b, last=False):
                        if not isinstance(t, int) or t > 0:
                            pool.wait_ge(xt_used, batches(t, s))
                        pool.tensor_copy(stage[:, 0:2 * D].rearrange("p (a d) -> p a d", a=1), big[:, at(t), :]).then_inc(copied, 1)
                        pool.tensor_copy(stage[:, 2 * D:3 * D].rearrange("p (a d) -> p a d", a=1), nodes[:, at(t), 0:D]).then_inc(copied, 1)
                        if not last:
                            ladder(t + 2, (b + 2) % BUFS)

                ladder(0, 0)
                ladder(1, 1)
                if s == 0:
                    add_columns(0, range(RING))
                tile(0, 0)
                tile(1, 1)
                with pool.Fori(0, BODY) as i:
                    for k in range(2, BUFS + 2):
                        tile(i * BUFS + k, k % BUFS)
                for t in range(T - 3, T):
                    tile(t, t % BUFS, last=t >= T - 2)

        @block.scalar
        def _(act):
            act.wait_ge(var_ready, 1)
            nc.scalar.activation(ln_b[:, :], ln_a[:, :], ACT.Sqrt).then_inc(std_ready, 1)
            act.wait_ge(affine_ready, 1)
            with act.Fori(0, T) as t:
                row = nodes[:, at(t), 0:D]
                act.activation(row, row, ACT.Relu, bias=ln_b[:, at(t)], scale=ln_a[:, at(t)]).then_inc(h_ready, 1)
            for s in range(2):
                def transposed(g):
                    for c in range(DC):
                        act.wait_ge(p_tr_full, g * 2 + (2 * NGROUP * s + c + 1))
                        act.activation(xt[:, c, :], tr[:, c, :], ACT.Copy).then_inc(p_xt_ready, 1)

                def project(g, last=False):
                    act.wait_ge(t1_full, g + (NGROUP * s + 1))
                    act.activation(t1, logits[0:DA, 0, BANK:2 * BANK], ACT.Copy).then_inc(t1_ready, 1)
                    act.wait_ge(k_full, g + (NGROUP * s + 1))
                    act.activation(k_stack[:, bass.ds(g * BANK, BANK)], logits[:, 0, 0:BANK], ACT.Copy).then_inc(kq_hi, 1)
                    if not last:
                        transposed(g + 1)
                    act.wait_ge(q_full, g + (NGROUP * s + 1))
                    act.activation(q_parts[:, 0, bass.ds(g * BANK, BANK)].bitcast(F32R), logits[:, 1, 0:BANK],
                                   ACT.Copy).then_inc(kq_hi, 1)

                transposed(0)
                with act.Fori(0, NGROUP - 1) as g:
                    project(g)
                project(NGROUP - 1, last=True)

                def exps(t, b):
                    act.wait_ge(negmax_ready, t + (T * s + 1))
                    act.activation(probs[:, b, :], probs[:, b, :], ACT.Exp, bias=negmax[:, b:b + 1], scale=-1.0,
                                   accum_out=zsum[:, b:b + 1]).then_inc(exp_done, 1)

                def weigh_point(t, b, k):
                    e = k // 2
                    if k % 2 == 0:
                        act.wait_ge(point_set, weighed(t, s) + (e + 1))
                        act.activation(dump[:, :], probs[:, b, :], ACT.Relu, bias=lad[:, b, 1, e:e + 1],
                                       accum_out=lad[:, b, 2, e:e + 1]).then_inc(relu_summed, 1)
                    else:
                        act.wait_ge(relu_summed, weighed(t, s) + (e + 1))
                        act.activation(dump[:, :], probs[:, b, :], ACT.Sign, bias=lad[:, b, 1, e:e + 1],
                                       accum_out=lad[:, b, 3, e:e + 1]).then_inc(point_weighed, 1)

                def to_sbuf(t, k):
                    act.wait_ge(tr_full, batches(t, s) + (k + 1))
                    act.wait_ge(xt_used, batches(t, s) + batch_free(k))
                    act.activation(xt[:, k % 2, :], tr[:, k % 2, :], ACT.Copy).then_inc(xt_ready, 1)

                def inverse_std(t):
                    act.wait_ge(var2_ready, t + 1)
                    act.activation(fin[:, 1:2], fin[:, 0:1], ACT.Ln).then_inc(log_done, 1)
                    act.wait_ge(log_done, t + 1)
                    act.activation(fin[:, 2:3], fin[:, 1:2], ACT.Exp, scale=-0.5).then_inc(rstd_ready, 1)

                def tile(t, b, last=False):
                    weighings = 0 if last else 2 * NLAD[s]
                    between = min(weighings, len(BETWEEN[s]))
                    for k in range(NTB):
                        to_sbuf(t, k)
                        if k == 0 and not last:
                            exps(t + 2, (b + 2) % BUFS)
                        if k == 1 and s and not (isinstance(t, int) and t == 0):
                            inverse_std(t - 1)
                        if between and k in BETWEEN[s]:
                            weigh_point(t + 2, (b + 2) % BUFS, BETWEEN[s].index(k))
                    act.wait_ge(xt_used, batches(t, s) + NTB)
                    if s == 0:
                        act.wait_ge(xa_stored, t * 16)
                        act.activation(xa_out[:, 0, :], acc[:, 0, :], ACT.Copy,
                                       scale=rkept[:, b:b + 1]).then_inc(xa_ready, 1)
                        act.wait_ge(xa_ready, t + 1)
                        act.dma_start(xa_dram[at(t), :, :], xa_out[:, 0, :]).then_inc(xa_stored, 16)
                    else:
                        act.activation(stage[:, 5 * D:6 * D], acc[:, 0, :], ACT.Copy,
                                       scale=rkept[:, b:b + 1]).then_inc(xa_ready, 1)
                        for k in range(NTB, NTB + UB):
                            to_sbuf(t, k)
                    for k in range(between, weighings):
                        weigh_point(t + 2, (b + 2) % BUFS, k)

                for t in range(2):
                    exps(t, t)
                    for k in range(2 * NLAD[s]):
                        weigh_point(t, t, k)
                tile(0, 0)
                tile(1, 1)
                with act.Fori(0, BODY) as i:
                    for k in range(2, BUFS + 2):
                        tile(i * BUFS + k, k % BUFS)
                for t in range(T - 3, T):
                    tile(t, t % BUFS, last=t >= T - 2)
                if s == 0:
                    act.wait_ge(cinv_ready, 1)
                    with act.Fori(0, T) as t:
                        act.activation(big[:, at(t), D:2 * D], big[:, at(t), 0:D], ACT.Copy,
                                       scale=cinv[:, at(t)]).then_inc(xb_ready, 1)
                else:
                    inverse_std(T - 1)

        @block.tensor
        def _(pe):
            pe.wait_ge(w_loaded, 16 * 13)
            pe.wait_ge(consts, 4)
            for s in range(2):
                def transpose_group(g, b):
                    pe.wait_ge(staged, g + (NGROUP * s + 1))
                    if not isinstance(g, int) or g > 0:
                        pe.wait_ge(p_xt_ready, g * 2 + NGROUP * s * 2)
                    for c in range(DC):
                        for j in range(GROUP):
                            ins = nc.tensor.transpose(tr[:, c, j * P:(j + 1) * P],
                                                      groups[b][:, j * D + c * P:j * D + (c + 1) * P], ident[:, :])
                        ins.then_inc(p_tr_full, 1)

                def project(g, b, last=False):
                    pe.wait_ge(p_xt_ready, g * 2 + (NGROUP * s * 2 + 2))
                    for c in range(DC):
                        ins = nc.tensor.matmul(logits[0:DA, 0, BANK:2 * BANK], w1[:, c, :], xt[:, c, :],
                                               start=c == 0, stop=c == DC - 1)
                    ins.then_inc(t1_full, 1)
                    if not isinstance(g, int) or g > 0:
                        pe.wait_ge(kq_done, g * 2 + NGROUP * s * 2)
                    for c in range(DC):
                        ins = nc.tensor.matmul(logits[:, 0, 0:BANK], w3d[:, c, :], xt[:, c, :], start=c == 0, stop=c == DC - 1)
                    ins.then_inc(k_full, 1)
                    if not last:
                        transpose_group(g + 1, 1 - b)
                    pe.wait_ge(t1_ready, g + (NGROUP * s + 1))
                    nc.tensor.matmul(logits[:, 1, 0:BANK], w2d[:, :], t1, start=True, stop=True).then_inc(q_full, 1)

                transpose_group(0, 0)
                project(0, 0)
                with pe.Fori(0, NGROUP // 2 - 1) as i:
                    for k in range(1, 3):
                        project(i * 2 + k, k % 2)
                project(NGROUP - 1, 1, last=True)
                pe.wait_ge(kq_done, (s + 1) * NGROUP * 2)
                if s == 1:
                    pe.wait_ge(big_ready, T)

                def logit_rows(t, b, nth, parts=range(LCH)):
                    pe.wait_ge(q_loaded[b], nth * 16 + loads(b, s) * 16)
                    for k in parts:
                        n = t * LCH + (T * s * LCH + k)
                        if not isinstance(t, int) or n >= 2:
                            pe.wait_ge(logits_free, n - 1)
                        for j in range(LW // BANK):
                            cols = slice(k * LW + j * BANK, k * LW + (j + 1) * BANK)
                            o = logits[:, k % 2, j * BANK:(j + 1) * BANK]
                            nc.tensor.matmul(o, q_tile[:, b, 0, :], k_stack[:, cols], start=True, stop=False)
                            ins = nc.tensor.matmul(o, q_tile[:, b, 1, :], k_stack[:, cols], start=False, stop=True)
                        ins.then_inc(logits_full, 1)

                def adj_rows(t):
                    pe.wait_ge(sx_read, t + T * s)
                    width = D + 1 if s == 0 else 2 * D
                    src = nodes if s == 0 else big
                    for k in range(NPIECE):
                        pe.wait_ge(adj_loaded[k % RING],
                                   t * (16 * NPIECE // RING) + (T * s * NPIECE // RING + k // RING + 1) * 16)
                        for c in range(PIECE):
                            ch = k * PIECE + c
                            ins = nc.tensor.matmul(sx[:, 0:width], adj_ring[:, k % RING, c, :], src[:, ch, 0:width],
                                                   start=ch == 0, stop=ch == T - 1)
                        ins.then_inc(adj_used, 1)

                def batch(t, k, block_of):
                    pe.wait_ge(xt_ready, batches(t, s) + batch_free(k))
                    for j in range(TB):
                        ins = nc.tensor.transpose(tr[:, k % 2, j * P:(j + 1) * P], block_of(k, j), ident[:, :])
                    ins.then_inc(tr_full, 1)

                def attend(t, b):
                    def block_of(k, j):
                        return probs[:, b, (k * TB + j) * P:(k * TB + j + 1) * P]

                    pe.wait_ge(masked, t + (T * s + 1))
                    batch(t, 0, block_of)
                    if not isinstance(t, int) or t + s > 0:
                        pe.wait_ge(xa_ready, t + T * s)
                    if s and not (isinstance(t, int) and t == 0):
                        pe.wait_ge(y_read, t)
                    for k in range(NTB):
                        if k + 1 < NTB:
                            batch(t, k + 1, block_of)
                        pe.wait_ge(xt_ready, batches(t, s) + (k + 1))
                        for j in range(TB):
                            ch = k * TB + j
                            ins = nc.tensor.matmul(acc[:, 0, :], xt[:, k % 2, j * P:(j + 1) * P], nodes[:, ch, 0:D],
                                                   start=ch == 0, stop=ch == T - 1)
                        ins.then_inc(xt_used, 1)

                def u_products(t):
                    def block_of(k, j):
                        n = (k - NTB) * TB + j
                        return stage[:, n * P:(n + 1) * P]

                    pe.wait_ge(copied, t * 2 + 2)
                    pe.wait_ge(sx_read, t + (T + 1))
                    pe.wait_ge(xa_ready, t + (T + 1))
                    batch(t, NTB, block_of)
                    for k in range(NTB, NTB + UB):
                        if k + 1 < NTB + UB:
                            batch(t, k + 1, block_of)
                        pe.wait_ge(xt_ready, batches(t, s) + (k + 1))
                        for j in range(TB):
                            n = (k - NTB) * TB + j
                            ins = nc.tensor.matmul(acc[:, 1, :], xt[:, k % 2, j * P:(j + 1) * P],
                                                   u_all[:, n // DC, n % DC, :], start=n == 0, stop=n == UB * TB - 1)
                        ins.then_inc(xt_used, 1)

                def tile(t, b, nth):
                    left = T - t if isinstance(t, int) else T
                    adj_rows(t)
                    if left > 2:
                        logit_rows(t + 2, (b + 2) % BUFS, nth + (b + 2) // BUFS, range(2, LCH))
                    attend(t, b)
                    if s:
                        u_products(t)
                    if left > 3:
                        logit_rows(t + 3, b, nth + 1, range(2))

                logit_rows(0, 0, 1)
                logit_rows(1, 1, 1)
                logit_rows(2, 2, 1, range(2))
                tile(0, 0, 1)
                tile(1, 1, 1)
                with pe.Fori(0, BODY) as i:
                    for k in range(2, BUFS + 2):
                        tile(i * BUFS + k, k % BUFS, i + (k // BUFS + 1))
                for t in range(T - 3, T):
                    tile(t, t % BUFS, t // BUFS + 1)

        @block.vector
        def _(dve):
            v = nc.vector
            seq = Chain(dve, dve_seq)

            def carry_wait():
                v.tensor_copy(pad[:, 1:2], pad[:, 0:1])

            def variance(mean, var, half, stat):
                v.tensor_tensor(mean, stat(1), stat(4), ALU.add)
                v.tensor_tensor(half, stat(1), stat(4), ALU.subtract)
                seq(v.tensor_tensor(var, stat(2), stat(5), ALU.add))
                v.tensor_scalar(mean, mean, 0.5, None, ALU.mult)
                v.tensor_scalar(var, var, 1.0 / D, EPS, ALU.mult, ALU.add)
                seq(v.scalar_tensor_tensor(out=half, in0=half, scalar=0.25, in1=half, op0=ALU.mult, op1=ALU.mult))
                return v.tensor_tensor(var, var, half, ALU.add)

            v.memset(flag[:, :], 0.0)
            seq(v.memset(pad[:, :], 0.0))
            for k in range(PARTS):
                dve.wait_ge(x_loaded[k], 16)
                with dve.Fori(k * T // PARTS, (k + 1) * T // PARTS) as t:
                    v.bn_stats(x_stats[:, at(t), :].rearrange("p a d -> p (a d)"),
                               nodes[:, at(t), 0:D].rearrange("p a d -> p (a d)")).then_inc(dve_seq, 1)
            seq.base, seq.k = T + 1, 0
            dve.wait_ge(dve_seq, T + 1)
            variance(x_mean, ln_a[:, :], ln_b[:, :], lambda k: x_stats[:, :, k]).then_inc(var_ready, 1)
            dve.wait_ge(std_ready, 1)
            seq(v.reciprocal(ln_c[:, :], ln_b[:, :]))
            seq(v.tensor_tensor(ln_b[:, :], ln_c[:, :], ln_c[:, :], ALU.mult))
            seq(v.tensor_tensor(ln_b[:, :], ln_b[:, :], ln_a[:, :], ALU.mult))
            seq(v.tensor_scalar(ln_b[:, :], ln_b[:, :], -0.5, 1.5, ALU.mult, ALU.add))
            seq(v.tensor_tensor(ln_a[:, :], ln_c[:, :], ln_b[:, :], ALU.mult))
            seq(v.tensor_tensor(ln_b[:, :], x_mean, ln_a[:, :], ALU.mult))
            v.tensor_scalar(ln_b[:, :], ln_b[:, :], -1.0, None, ALU.mult).then_inc(affine_ready, 1)

            for s in range(2):
                with dve.Fori(0, NGROUP) as g:
                    kcols = bass.ds(g * BANK, BANK)
                    dve.wait_ge(kq_hi, g * 2 + (NGROUP * s * 2 + 1))
                    v.tensor_tensor(k_stack[DA:P, kcols], logits[DA:P, 0, 0:BANK], k_stack[DA:P, kcols].bitcast(F32),
                                    ALU.subtract).then_inc(kq_done, 1)
                    dve.wait_ge(kq_hi, g * 2 + (NGROUP * s * 2 + 2))
                    v.tensor_tensor(q_parts[:, 1, kcols].bitcast(F32R), logits[:, 1, 0:BANK], q_parts[:, 0, kcols],
                                    ALU.subtract).then_inc(kq_done, 1)

                def evacuate(t, b, parts=range(LCH)):
                    for k in parts:
                        dve.wait_ge(logits_full, t * LCH + (T * s * LCH + k + 1))
                        v.tensor_scalar(probs[:, b, k * LW:(k + 1) * LW], logits[:, k % 2, :], -1.0, None, ALU.mult,
                                        ALU.min, accum_out=part_min[:, b, k:k + 1]).then_inc(logits_free, 1)
                    if LCH - 1 in parts:
                        dve.wait_ge(logits_free, t * LCH + (T * s + 1) * LCH)
                        v.tensor_reduce(negmax[:, b:b + 1], part_min[:, b, :], AX_X, ALU.min).then_inc(negmax_ready, 1)

                def finish(t):
                    dve.wait_ge(xt_used, batches(t + 1, 1))
                    dve.wait_ge(hx_loaded, (t + 1) * 32)
                    v.tensor_tensor(y_t, acc[:, 1, :], h_in, ALU.add).then_inc(y_read, 1)
                    dve.wait_ge(y_read, t + 1)
                    seq(v.bn_stats(bn[:, :], y_t))
                    variance(fin[:, 4:5], fin[:, 0:1], fin[:, 3:4], lambda k: bn[:, k:k + 1]).then_inc(var2_ready, 1)

                def finish_rest(t):
                    dve.wait_ge(rstd_ready, t + 1)
                    v.tensor_tensor(x_in, x_in, bet[:, :], ALU.add)
                    seq(v.tensor_scalar(fin[:, 3:4], fin[:, 2:3], fin[:, 2:3], fin[:, 0:1], ALU.mult, ALU.mult))
                    seq(v.tensor_scalar(fin[:, 3:4], fin[:, 3:4], -0.5, 1.5, ALU.mult, ALU.add))
                    seq(v.tensor_scalar(fin[:, 3:4], fin[:, 3:4], fin[:, 2:3], None, ALU.mult))
                    seq(v.tensor_scalar(y_t, y_t, fin[:, 4:5], fin[:, 3:4], ALU.subtract, ALU.mult))
                    seq(v.tensor_tensor(y_t, y_t, gam[:, :], ALU.mult))
                    v.tensor_tensor(x_in, y_t, x_in, ALU.add).then_inc(o_ready, 1)

                def start_search(b):
                    n = NLAD[s]
                    x = lad[:, b, 0, 0:n]
                    mass, up, down = (lad_v[:, k, 0:n] for k in range(3))
                    whole = zsum[:, b:b + 1]
                    v.tensor_scalar(ends[:, 0, n:n + 1], whole, 0.99 * (1 - P_NUC) / N, None, ALU.mult)
                    v.memset(ends[:, 1, n:n + 1], TOP)
                    v.tensor_scalar(ends[:, 2, n:n + 1], whole, 1 - P_NUC, None, ALU.mult)
                    v.tensor_scalar(ends[:, 3, n:n + 1], whole, -P_NUC, None, ALU.mult)
                    v.tensor_scalar(target, whole, P_NUC, None, ALU.mult)
                    v.tensor_scalar(slack, whole, 1 - P_NUC * (1 + SLACK), None, ALU.mult)
                    seq(v.tensor_scalar(mass, lad[:, b, 3, 0:n], 0.5, N / 2, ALU.mult, ALU.add))
                    v.tensor_scalar(up, lad[:, b, 2, 0:n], target, None, ALU.subtract)
                    seq(v.tensor_tensor(mass, mass, x, ALU.mult))
                    seq(v.tensor_tensor(mass, mass, up, ALU.add))
                    v.tensor_scalar(up, mass, 0.0, None, ALU.is_ge)
                    seq(v.tensor_scalar(down, mass, 0.0, None, ALU.is_lt))
                    v.tensor_tensor(ends[:, 0, 0:n], up, x, ALU.mult)
                    v.scalar_tensor_tensor(out=ends[:, 1, 0:n], in0=up, scalar=2.0, in1=x, op0=ALU.mult, op1=ALU.add)
                    v.scalar_tensor_tensor(out=ends[:, 2, 0:n], in0=down, scalar=FAR, in1=mass, op0=ALU.mult, op1=ALU.add)
                    seq(v.scalar_tensor_tensor(out=ends[:, 3, 0:n], in0=up, scalar=-FAR, in1=mass, op0=ALU.mult, op1=ALU.add))
                    v.tensor_reduce(lo[:, 0:1], ends[:, 0, 0:n + 1], AX_X, ALU.max)
                    v.tensor_reduce(hi[:, 0:1], ends[:, 1, 0:n + 1], AX_X, ALU.min)
                    v.tensor_reduce(lo[:, 1:2], ends[:, 2, 0:n + 1], AX_X, ALU.min)
                    seq(v.tensor_reduce(hi[:, 1:2], ends[:, 3, 0:n + 1], AX_X, ALU.max))
                    next_point(seq)

                def next_point(q, edge=EDGE):
                    v.scalar_tensor_tensor(out=numer, in0=lo[:, 0:1], scalar=-AIM, in1=lo[:, 1:2], op0=ALU.mult, op1=ALU.subtract)
                    q(v.tensor_tensor(gap, hi[:, 0:2], lo[:, 0:2], ALU.subtract))
                    v.reciprocal(ratio, gap[:, 1:2])
                    v.tensor_tensor(way, numer, gap[:, 0:1], ALU.mult)
                    v.scalar_tensor_tensor(out=least, in0=gap[:, 0:1], scalar=edge, in1=lo[:, 0:1], op0=ALU.mult, op1=ALU.add)
                    q(v.scalar_tensor_tensor(out=most, in0=gap[:, 0:1], scalar=1 - edge, in1=lo[:, 0:1], op0=ALU.mult, op1=ALU.add))
                    q.mark(v.tensor_scalar(way, way, ratio, lo[:, 0:1], ALU.mult, ALU.add))
                    v.tensor_scalar(lo[:, 1:2], lo[:, 1:2], FADE, None, ALU.mult)
                    v.tensor_scalar(hi[:, 1:2], hi[:, 1:2], FADE, None, ALU.mult)
                    q.wait()
                    q(v.tensor_scalar(new[:, 0:1], way, least, most, ALU.max, ALU.min))

                def weigh(b, q, edge=EDGE):
                    q(v.scalar_tensor_tensor(out=scratch[:, :], in0=probs[:, b, :], scalar=new[:, 0:1],
                                             in1=probs[:, b, :], op0=ALU.is_ge, op1=ALU.mult, accum_out=new[:, 2:3]))
                    mass = new[:, 2:3].to_broadcast([P, 2])
                    v.tensor_scalar(reaches[:, :], mass, target, None, ALU.is_ge)
                    v.tensor_scalar(misses[:, :], mass, target, None, ALU.is_lt)
                    q(v.tensor_tensor(new[:, 1:2], new[:, 2:3], target, ALU.subtract))
                    carry_wait()
                    v.copy_predicated(lo[:, :], reaches[:, :], new[:, 0:2])
                    q(v.copy_predicated(hi[:, :], misses[:, :], new[:, 0:2]))
                    next_point(q, edge)

                def settle(b, q, check=True):
                    q(v.scalar_tensor_tensor(out=scratch[:, :], in0=probs[:, b, :], scalar=hi[:, 0:1],
                                             in1=probs[:, b, :], op0=ALU.is_lt, op1=ALU.mult, accum_out=below))
                    if check:
                        v.tensor_scalar(ratio, below, slack, -FAR, ALU.is_le, ALU.mult)
                    q.mark(v.tensor_tensor(upper, zsum[:, b:b + 1], below, ALU.subtract))
                    if check:
                        v.max(best[:, 0:8], scratch[:, :])
                        q.wait()
                        q(v.tensor_tensor(upper, upper, ratio, ALU.add))
                    else:
                        q(v.max(best[:, 0:8], scratch[:, :]))
                    v.tensor_copy(best[:, 8:9], best[:, 7:8])
                    q(v.tensor_tensor_scan(best_sum[:, :], best[:, 0:8], best[:, 0:8], upper, ALU.add, ALU.max))
                    v.tensor_copy(best_ok[:, 8:9], best[:, 8:9])
                    q(v.scalar_tensor_tensor(out=best_ok[:, 0:8], in0=best_sum[:, :], scalar=target, in1=best[:, 0:8],
                                             op0=ALU.is_ge, op1=ALU.mult))
                    q(v.reduce_max(thr, best_ok[:, :], AX_X))
                    v.tensor_scalar(best_ok[:, :], best[:, :], thr, None, ALU.is_equal, ALU.add, accum_out=flag[:, 0:1])
                    v.tensor_scalar(negthr, thr, -1.0, None, ALU.mult)
                    q(v.scalar_tensor_tensor(out=best_sum[:, :], in0=best[:, 0:8], scalar=thr, in1=best[:, 0:8],
                                             op0=ALU.is_gt, op1=ALU.mult, accum_out=above))
                    q(v.tensor_tensor(above, above, upper, ALU.add))

                def any_flag(q):
                    q(v.transpose(flag_t[:, :], flag[:, :]))
                    q(v.reduce_max(flag_q[:, 0:1], flag_t[:, :], AX_X))
                    v.tensor_copy(flag_q[0:32, 1:2], flag_q[32:64, 0:1])
                    v.tensor_copy(flag_q[0:32, 2:3], flag_q[64:96, 0:1])
                    q(v.tensor_copy(flag_q[0:32, 3:4], flag_q[96:128, 0:1]))
                    q(v.reduce_max(flag_i[0:32, :], flag_q[0:32, :], AX_X))
                    carry_wait()
                    return dve.value_load(flag_i[0:1, 0:1], min_val=0, max_val=9)

                def ties(b, q):
                    v.reciprocal(ratio, thr)
                    q(v.tensor_scalar(tied, probs[:, b, :], thr, None, ALU.is_equal))
                    q(v.tensor_scalar(numer, target, above, ratio, ALU.subtract, ALU.mult))
                    q(v.tensor_tensor_scan(rank, tied, tied, 0.0, ALU.add, ALU.max))
                    v.tensor_scalar(limit, numer, 1.0, 1.5, ALU.add, ALU.max)
                    q(v.scalar_tensor_tensor(out=flag[:, 0:1], in0=numer, scalar=-ROOM, in1=rank[:, N - 1:N],
                                             op0=ALU.add, op1=ALU.is_gt))

                def drop_ties(b, q):
                    q(v.scalar_tensor_tensor(out=tied, in0=rank, scalar=limit, in1=tied, op0=ALU.is_ge, op1=ALU.mult))
                    q(v.scalar_tensor_tensor(out=probs[:, b, :], in0=tied, scalar=negthr, in1=probs[:, b, :],
                                             op0=ALU.mult, op1=ALU.add))

                def again(b):
                    rnd = Chain(dve, round_seq)
                    v.tensor_scalar(reaches[:, :], upper.to_broadcast([P, 2]), 0.0, None, ALU.is_lt)
                    v.memset(new[:, 0:1], TOP)
                    rnd(v.tensor_scalar(new[:, 1:2], target, -1.0, None, ALU.mult))
                    rnd(v.copy_predicated(hi[:, :], reaches[:, :], new[:, 0:2]))
                    next_point(rnd)
                    for n in range(ROUND_PASSES):
                        weigh(b, rnd, edge=0.5 if n == ROUND_PASSES - 2 else EDGE)
                    settle(b, rnd, check=False)
                    ties(b, rnd)
                    any_flag(rnd)
                    dve.sem_clear(round_seq)

                def resolve(b, q):
                    ties(b, q)
                    with dve.If(any_flag(q) > 0):
                        again(b)
                        with dve.If(dve.value_load(flag_i[0:1, 0:1], min_val=0, max_val=9) > 0):
                            with dve.Fori(0, ROUNDS):
                                with dve.If(dve.value_load(flag_i[0:1, 0:1], min_val=0, max_val=9) > 0):
                                    again(b)
                    drop_ties(b, q)

                def read_adj_product(t, first):
                    dve.wait_ge(adj_used, (t + 1) * NPIECE + T * s * NPIECE)
                    if s == 0:
                        seq(v.tensor_tensor(big[:, at(t), 0:D].rearrange("p a d -> p (a d)"), sx[:, 0:D],
                                            nodes[:, at(t), 0:D].rearrange("p a d -> p (a d)"), ALU.add))
                        v.tensor_scalar(rinv[:, at(t)], sx[:, D:D + 1], 1.0, 1e-12, ALU.add, ALU.max)\
                            .then_inc(sx_read, 1)
                        return
                    if not first:
                        dve.wait_ge(xt_used, batches(t, s))
                    seq(v.tensor_tensor(stage[:, 3 * D:5 * D], sx[:, :],
                                        big[:, at(t), :].rearrange("p a d -> p (a d)"), ALU.add))
                    seq(v.tensor_scalar(stage[:, 3 * D:4 * D], stage[:, 3 * D:4 * D], rinv[:, at(t)], None, ALU.mult))
                    v.tensor_scalar(stage[:, 4 * D:5 * D], stage[:, 4 * D:5 * D], cinv[:, at(t)], None, ALU.mult)\
                        .then_inc(sx_read, 1)

                def mask(t, b):
                    settle(b, seq)
                    if s == 0:
                        with dve.If(any_flag(seq) > 1):
                            tie = Chain(dve, tie_seq)
                            resolve(b, tie)
                            dve.sem_clear(tie_seq)
                    else:
                        resolve(b, seq)
                    seq(v.scalar_tensor_tensor(out=probs[:, b, :], in0=probs[:, b, :], scalar=thr, in1=probs[:, b, :],
                                               op0=ALU.is_ge, op1=ALU.mult, accum_out=kept))
                    v.reciprocal(rkept[:, b:b + 1], kept).then_inc(masked, 1)

                def tile(t, b, last=False):
                    early = t if isinstance(t, int) else T
                    dve.wait_ge(point_weighed, weighed(t + 1, s))
                    start_search(b)
                    half = PASSES[s] // 2
                    for _ in range(PASSES[s] - half):
                        weigh(b, seq)
                    if s and early >= 2:
                        finish_rest(t - 2)
                    for _ in range(half):
                        weigh(b, seq)
                    if s and early >= 1:
                        finish(t - 1)
                    mask(t, b)
                    if not last:
                        if early >= 1:
                            dve.wait_ge(tr_full, batches(t, s) - (UB if s else 0))
                        evacuate(t + 2, (b + 2) % BUFS, range(2))
                    read_adj_product(t, early == 0)
                    if not last:
                        evacuate(t + 2, (b + 2) % BUFS, range(2, LCH))

                evacuate(0, 0)
                evacuate(1, 1)
                tile(0, 0)
                tile(1, 1)
                seq.base, seq.k = seq.base + seq.k, 0
                base = seq.base
                per = SEQ_PER_TILE[s]
                with dve.Fori(0, BODY) as i:
                    seq.base, seq.k = i * (BUFS * per) + base, 0
                    for k in range(BUFS):
                        tile(i * BUFS + (k + 2), (k + 2) % BUFS)
                        assert seq.k == (k + 1) * per, seq.k
                seq.base, seq.k = base + BODY * BUFS * per, 0
                for t in range(T - 3, T):
                    tile(t, t % BUFS, last=t >= T - 2)
                if s == 0:
                    dve.wait_ge(cols_added, T * NPIECE)
                    seq(v.reduce_sum(cinv[:, :], big[:, :, D:D + P], AX_X))
                    seq(v.tensor_scalar(cinv[:, :], cinv[:, :], 1.0, 1e-12, ALU.add, ALU.max))
                    seq(v.reciprocal(rinv[:, :], rinv[:, :]))
                    v.reciprocal(cinv[:, :], cinv[:, :]).then_inc(cinv_ready, 1)
                    with dve.Fori(0, T) as t:
                        dve.wait_ge(xb_ready, t + 1)
                        v.tensor_scalar(big[:, at(t), 0:D], big[:, at(t), 0:D], rinv[:, at(t)], None, ALU.mult)\
                            .then_inc(big_ready, 1)
                else:
                    finish_rest(T - 2)
                    finish(T - 1)
                    finish_rest(T - 1)


def kernel(x, adj, L0_gnn_W1, L0_gnn_W2, L0_gnn_W3, L0_gnn_U1, L0_gnn_U2, L0_gnn_U3, L0_gnn_gamma, L0_gnn_beta):
    import concourse.bacc as bacc
    from concourse.bass_utils import run_bass_kernel_spmd

    def arr(a):
        return np.ascontiguousarray(np.asarray(a))

    arrays = {
        "x_in_dram": arr(x),
        "adj_t_dram": arr(np.asarray(adj).reshape(T, P, T, P).transpose(0, 3, 2, 1)),
        "w1_dram": arr(L0_gnn_W1), "w2_dram": arr(L0_gnn_W2), "w3_dram": arr(L0_gnn_W3),
        "u1_dram": arr(L0_gnn_U1), "u2_dram": arr(L0_gnn_U2), "u3_dram": arr(L0_gnn_U3),
        "gamma_dram": arr(np.broadcast_to(np.asarray(L0_gnn_gamma), (P, D))),
        "beta_dram": arr(np.broadcast_to(np.asarray(L0_gnn_beta), (P, D))),
    }
    nc = bacc.Bacc("TRN2", target_bir_lowering=False, num_devices=1, dynamic_dma_scratch_size=2048)
    args = [nc.dram_tensor(n, a.shape, mybir.dt.from_np(a.dtype), kind="ExternalInput").ap()
            for n, a in arrays.items()]
    out = nc.dram_tensor("out_dram", (N, D), F32, kind="ExternalOutput").ap()
    build(nc, *args, out)
    r = run_bass_kernel_spmd(nc, [arrays], core_ids=[0])
    return r.results[0]["out_dram"]
```
